# Optimizing a Trainium2 kernel written in Bass

```python
import numpy as np
import jax
import jax.numpy as jnp

def _softmax(x, axis=-1):
    return jax.nn.softmax(x, axis=axis)

def _gelu(x):
    return jax.nn.gelu(x, approximate=True)

def _silu(x):
    return jax.nn.silu(x)

def _sigmoid(x):
    return jax.nn.sigmoid(x)

def _layernorm(x, axis=-1, eps=1e-05):
    m = jnp.mean(x, axis=axis, keepdims=True)
    v = jnp.var(x, axis=axis, keepdims=True)
    return (x - m) / jnp.sqrt(v + eps)

def _scatter_add(tgt, idx, src, axis=0):
    return tgt.at[idx].add(src)

def _segment_sum(src, seg, n):
    return jax.ops.segment_sum(src, seg, n)
kernel_name = 'mk_macaron_d1_jaxref_r8_0dc3fc'

def setup_inputs(seed: int=0):
    np.random.seed(seed)
    _w = jnp.asarray

    def _L0_attn_setup():
        import jax, jax.numpy as jnp
        import numpy as np
        HIDDEN = 128
        NUM_HEADS = 16
        HEAD_DIM = HIDDEN // NUM_HEADS
        WINDOW = 512

        def _sliding_window_mask(seq_len, window_size):
            return jnp.ones((seq_len, seq_len), dtype=jnp.float32)
        key = jax.random.key(seed)
        ks = jax.random.split(key, 5)
        B, S = (2, 256)
        hidden_states = jax.random.normal(ks[0], (B, S, HIDDEN), dtype=jnp.float32)
        scale = 1.0 / np.sqrt(HIDDEN)
        Wq = jax.random.normal(ks[1], (HIDDEN, HIDDEN), dtype=jnp.float32) * scale
        Wk = jax.random.normal(ks[2], (HIDDEN, HIDDEN), dtype=jnp.float32) * scale
        Wv = jax.random.normal(ks[3], (HIDDEN, HIDDEN), dtype=jnp.float32) * scale
        Wo = jax.random.normal(ks[4], (HIDDEN, HIDDEN), dtype=jnp.float32) * scale
        return {'hidden_states': hidden_states, 'Wq': Wq, 'Wk': Wk, 'Wv': Wv, 'Wo': Wo}
    _L0_attn_in = _L0_attn_setup()

    def _L0_ffn_setup():
        import jax, jax.numpy as jnp
        import numpy as np
        TOP_K = 2
        NUM_EXPERTS = 8
        DIM = 128
        HIDDEN = 352
        BS, SLEN = (2, 128)

        def _grouped_ffn(x, w1, w2, w3, counts):
            num_experts = w1.shape[0]
            ends = jnp.cumsum(counts)
            starts = ends - counts
            t = jnp.arange(x.shape[0])
            out = jnp.zeros((x.shape[0], w2.shape[-1]), x.dtype)
            for e in range(num_experts):
                m = ((t >= starts[e]) & (t < ends[e])).astype(x.dtype)[:, None]
                xe = x * m
                h = jax.nn.silu(xe @ w1[e]) * (xe @ w3[e])
                out = out + h @ w2[e] * m
            return out
        key = jax.random.key(seed)
        k = jax.random.split(key, 5)
        std = 0.02
        return {'x': jax.random.normal(k[0], (BS, SLEN, DIM), jnp.float32), 'gate_w': jax.random.normal(k[1], (NUM_EXPERTS, DIM), jnp.float32) * std, 'expert_bias': jnp.zeros((NUM_EXPERTS,), jnp.float32), 'w1': jax.random.normal(k[2], (NUM_EXPERTS, DIM, HIDDEN), jnp.float32) * std, 'w2': jax.random.normal(k[3], (NUM_EXPERTS, HIDDEN, DIM), jnp.float32) * std, 'w3': jax.random.normal(k[4], (NUM_EXPERTS, DIM, HIDDEN), jnp.float32) * std}
    _L0_ffn_in = _L0_ffn_setup()
    _d = {'L0_attn_hidden_states': _L0_attn_in['hidden_states'], 'L0_attn_Wq': _L0_attn_in['Wq'], 'L0_attn_Wk': _L0_attn_in['Wk'], 'L0_attn_Wv': _L0_attn_in['Wv'], 'L0_attn_Wo': _L0_attn_in['Wo'], 'L0_ffn_gate_w': _L0_ffn_in['gate_w'], 'L0_ffn_expert_bias': _L0_ffn_in['expert_bias'], 'L0_ffn_w1': _L0_ffn_in['w1'], 'L0_ffn_w2': _L0_ffn_in['w2'], 'L0_ffn_w3': _L0_ffn_in['w3']}
    _x0 = _d['L0_attn_hidden_states']
    _d['L0_attn_hidden_states'] = jax.random.normal(jax.random.fold_in(jax.random.key(seed), 1), (16, 256, 128), dtype=_x0.dtype)
    del _x0
    return _d

def reference(L0_attn_hidden_states, L0_attn_Wq, L0_attn_Wk, L0_attn_Wv, L0_attn_Wo, L0_ffn_gate_w, L0_ffn_expert_bias, L0_ffn_w1, L0_ffn_w2, L0_ffn_w3):

    def _L0_attn_ref(hidden_states, Wq, Wk, Wv, Wo):
        import jax, jax.numpy as jnp
        import numpy as np
        HIDDEN = 128
        NUM_HEADS = 16
        HEAD_DIM = HIDDEN // NUM_HEADS
        WINDOW = 512

        def _sliding_window_mask(seq_len, window_size):
            return jnp.ones((seq_len, seq_len), dtype=jnp.float32)
        B, S, H = hidden_states.shape
        nH, hd = (NUM_HEADS, HEAD_DIM)

        def proj(W):
            y = jnp.einsum('bsh,oh->bso', hidden_states, W)
            return y.reshape(B, S, nH, hd).transpose(0, 2, 1, 3)
        q, k, v = (proj(Wq), proj(Wk), proj(Wv))
        scores = jnp.einsum('bnsd,bntd->bnst', q, k) / np.sqrt(hd)
        mask = _sliding_window_mask(S, WINDOW)
        scores = jnp.where(mask == 0, -jnp.inf, scores)
        attn = jax.nn.softmax(scores, axis=-1)
        out = jnp.einsum('bnst,bntd->bnsd', attn, v)
        out = out.transpose(0, 2, 1, 3).reshape(B, S, H)
        return jnp.einsum('bsh,oh->bso', out, Wo)

    def _L0_ffn_ref(x, gate_w, expert_bias, w1, w2, w3):
        import jax, jax.numpy as jnp
        import numpy as np
        TOP_K = 2
        NUM_EXPERTS = 8
        DIM = 128
        HIDDEN = 352
        BS, SLEN = (2, 128)

        def _grouped_ffn(x, w1, w2, w3, counts):
            num_experts = w1.shape[0]
            ends = jnp.cumsum(counts)
            starts = ends - counts
            t = jnp.arange(x.shape[0])
            out = jnp.zeros((x.shape[0], w2.shape[-1]), x.dtype)
            for e in range(num_experts):
                m = ((t >= starts[e]) & (t < ends[e])).astype(x.dtype)[:, None]
                xe = x * m
                h = jax.nn.silu(xe @ w1[e]) * (xe @ w3[e])
                out = out + h @ w2[e] * m
            return out
        bs, slen, dim = x.shape
        num_experts = gate_w.shape[0]
        xf = x.reshape(bs * slen, dim)
        scores = jax.nn.softmax((xf @ gate_w.T).astype(jnp.float32), axis=-1)
        _, sel = jax.lax.top_k(scores + expert_bias, TOP_K)
        top_scores = jnp.take_along_axis(scores, sel, axis=1).reshape(-1)
        sel_flat = sel.reshape(-1)
        counts = jnp.zeros((num_experts,), jnp.int32).at[sel_flat].add(1)
        order = jnp.argsort(sel_flat, stable=True)
        top_scores_sorted = top_scores[order]
        token_idx = order // TOP_K
        routed = xf[token_idx] * top_scores_sorted[:, None].astype(xf.dtype)
        routed_out = _grouped_ffn(routed, w1, w2, w3, counts)
        out = jnp.zeros_like(xf).at[token_idx].add(routed_out)
        return out.reshape(bs, slen, dim)
    x = L0_attn_hidden_states
    x = x + 0.5 * _L0_ffn_ref(_layernorm(x, axis=-1), L0_ffn_gate_w, L0_ffn_expert_bias, L0_ffn_w1, L0_ffn_w2, L0_ffn_w3)
    x = x + _L0_attn_ref(_layernorm(x, axis=-1), L0_attn_Wq, L0_attn_Wk, L0_attn_Wv, L0_attn_Wo)
    x = x + 0.5 * _L0_ffn_ref(_layernorm(x, axis=-1), L0_ffn_gate_w, L0_ffn_expert_bias, L0_ffn_w1, L0_ffn_w2, L0_ffn_w3)
    return x

_drawn_inputs = setup_inputs


def setup_inputs(seed=0):
    import zlib

    import numpy as np

    out = dict(_drawn_inputs(seed))
    spreads = {'L0_ffn_expert_bias': (0.0, 0.8)}
    factors = {'L0_ffn_gate_w': 8.0, 'L0_ffn_w1': 8.0, 'L0_ffn_w2': 8.0, 'L0_ffn_w3': 8.0}
    for name, (base, spread) in spreads.items():
        noise = np.random.default_rng([zlib.crc32(name.encode()), seed]).standard_normal(out[name].shape)
        drawn = base * np.exp(spread * noise) if base else spread * noise
        out[name] = jnp.asarray(drawn.astype(out[name].dtype))
    for name, factor in factors.items():
        out[name] = (out[name] * factor).astype(out[name].dtype)
    return out
```

```python
from contextlib import ExitStack

import concourse.bass as bass
import numpy as np
from concourse import mybir

P = 128
BATCH, SEQ, D = 16, 256, 128
HEADS, HD = 16, 8
PAIRS = HEADS // 2
EXPERTS, HIDDEN, TOP_K = 8, 352, 2
TILES = BATCH * SEQ // P
HALVES = 2
TH = TILES // HALVES
NB = BATCH // HALVES
NT = TOP_K * TH + EXPERTS - 1
HC = -(-HIDDEN // P)
HP = HC * P
LN_EPS = 1e-5
FAR = 1e30
ROUNDS = 2

LOOPS = False
RING = 4
TERMS = ((0, 0), (1, 1), (2, 0), (0, 1), (1, 0), (0, 2))
NTERM = len(TERMS)
STACK = 2 * HD * NTERM

F32, BF16, I32 = mybir.dt.float32, mybir.dt.bfloat16, mybir.dt.int32
ALU, ACT, AX = mybir.AluOpType, mybir.ActivationFunctionType, mybir.AxisListType

C_ID, C_BEFORE, C_ONES = 0, P, 2 * P
C_REV = 3 * P
C_STEP = C_REV + EXPERTS
C_TILE = C_STEP + TH
C_SEG = C_TILE + NT
C_END = C_SEG + EXPERTS * TH


def constants():
    c = np.zeros((P, C_END), np.float32)
    c[:, C_ID:C_ID + P] = np.eye(P)
    c[:, C_BEFORE:C_BEFORE + P] = np.triu(np.ones((P, P)), 1)
    c[:, C_ONES:C_ONES + P] = 1
    c[:, C_REV:C_STEP] = EXPERTS - np.arange(EXPERTS)
    c[:, C_STEP:C_TILE] = P * np.arange(TH)
    c[:, C_TILE:C_SEG] = np.arange(NT)
    c[:, C_SEG:] = np.tile(np.arange(TH) > 0, EXPERTS)
    return c


def wait(eng, sem, value):
    if not isinstance(value, int) or value > 0:
        eng.wait_ge(sem, value)


def steps(eng, first, last, low, high, body, unroll=2):
    high = low + (high - low) // unroll * unroll
    for i in range(first, low):
        body(i, i % unroll, i // unroll)
    if LOOPS:
        with eng.Fori(low // unroll, high // unroll) as j:
            for r in range(unroll):
                body(unroll * j + r, r, j)
    else:
        high = low
    for i in range(high, last):
        body(i, i % unroll, i // unroll)


def at(view, i):
    return view[:, bass.ds(i, 1)]


def one(view, i):
    return at(view, i).squeeze(1)


def build(nc, x, wq, wk, wv, wo, gate, bias, w1, w2, w3, consts, out, stop=None):
    with ExitStack() as ctx:
        def sb(name, shape, dt=F32):
            return ctx.enter_context(nc.sbuf_tensor(name, shape, dt))

        def sem(name):
            return ctx.enter_context(nc.semaphore(name))

        X = sb("X", [P, TILES, D])
        CT = sb("CT", [P, C_END])
        W1 = sb("W1", [P, EXPERTS, HIDDEN])
        W3 = sb("W3", [P, EXPERTS, HIDDEN])
        W2 = sb("W2", [P, EXPERTS, HC, D])
        GATE = sb("GATE", [P, EXPERTS])
        BIAS = sb("BIAS", [P, EXPERTS])
        ident = CT[:, C_ID:C_ID + P]
        ones = CT[:, C_ONES:C_ONES + P]

        stats6 = sb("stats6", [P, TH, 6])
        mean, var, rstd = sb("mean", [P, TH]), sb("var", [P, TH]), sb("rstd", [P, TH])
        msum, mdiff, msq, rough, rr = (sb(n, [P, TH]) for n in ("msum", "mdiff", "msq", "rough", "rr"))
        half_power = sb("half_power", [P, TH])

        xr = sb("xr", [P, 2, D])
        xrT = sb("xrT", [P, 2, P])
        te3 = [P, TH, EXPERTS]
        shifted, weight, score = sb("shifted", te3), sb("weight", te3), sb("score", te3)
        biased, found = sb("biased", te3), sb("found", te3)
        chosen = sb("chosen", [P, TOP_K, TH, EXPERTS])
        picked = sb("picked", [P, TOP_K, TH, EXPERTS])
        colmax, total = sb("colmax", [P, TH]), sb("total", [P, TH])
        coef = sb("coef", [P, TOP_K, TH])
        et3 = [P, EXPERTS, TH]
        taken, upto, place = sb("taken", et3), sb("upto", et3), sb("place", et3)
        rowsum = sb("rowsum", [P, EXPERTS])
        tiles_of, last_tile, start = (sb(n, [P, EXPERTS]) for n in ("tiles_of", "last_tile", "start"))
        over = sb("over", [P, EXPERTS, TH])
        passed = sb("passed", [P, NT, EXPERTS])
        slot_f = sb("slot_f", [P, TOP_K, TH])
        slot = [sb(f"slot{h}", [P, TOP_K, TH], I32) for h in range(HALVES)]
        expert_f = sb("expert_f", [P, NT])
        expert = [sb(f"expert{h}", [P, NT], I32) for h in range(HALVES)]
        rows = [sb(f"rows{h}", [P, TOP_K, TH, D]) for h in range(HALVES)]

        xe = sb("xe", [P, RING, D])
        xeT = sb("xeT", [P, 2, P])
        act1 = sb("act1", [P, 2, HIDDEN])
        hid = sb("hid", [P, 2, HP])
        hidT = sb("hidT", [P, 2, HP])
        ye = sb("ye", [P, RING, D])
        zeros = sb("zeros", [P, NT * 32])

        slots_in = [nc.dram_tensor(f"slots_in{h}", [NT * P, D], F32).ap() for h in range(HALVES)]
        slots_out = [nc.dram_tensor(f"slots_out{h}", [NT * P, D], F32).ap() for h in range(HALVES)]

        WQ, WK, WV, WO = (sb(n, [P, D]) for n in ("WQ", "WK", "WV", "WO"))
        identb = sb("identb", [P, P], BF16)
        xa, xaT = sb("xa", [P, 2, D]), sb("xaT", [P, SEQ])
        split = sb("split", [P, 2, 3, SEQ], BF16)
        resid = sb("resid", [P, 2, SEQ])
        QS = [sb(f"QS{q}", [P, PAIRS, 2, SEQ], BF16) for q in range(2)]
        KS = [sb(f"KS{q}", [P, PAIRS, SEQ], BF16) for q in range(2)]
        zrows = sb("zrows", [4, 4 * 2 * SEQ], BF16)
        V1 = [sb(f"V1_{q}", [P, 2, HEADS, 32]) for q in range(3)]
        PT = sb("PT", [P, 2, 2, 2, SEQ])
        mx = sb("mx", [P, 2, 2, PAIRS])
        nm = sb("nm", [P, 2, 4 * PAIRS], BF16)
        nmT = sb("nmT", [4 * PAIRS, SEQ], BF16)
        oT = sb("oT", [P, HEADS // 4, SEQ])
        rsum, on = sb("rsum", [P, 2, HEADS]), sb("on", [P, 2, D])
        onT = sb("onT", [P, SEQ])
        scratch = nc.dram_tensor("stacks", [2, 2, 2, PAIRS, HD, NTERM, SEQ], BF16).ap()

        banks = ctx.enter_context(nc.psum_tensor("banks", [P, 8, 512], F32))
        PS = [banks[:, b, :] for b in range(8)]
        ST = [banks[:, 2 * b:2 * b + 2, :].rearrange("p b n -> p (b n)") for b in range(2)]

        s_x = [sem(f"s_x{h}") for h in range(HALVES)]
        s_const = sem("s_const")
        s_w = sem("s_w")
        s_cleared = [sem(f"s_cleared{h}") for h in range(HALVES)]
        s_zero = sem("s_zero")
        s_dve = sem("s_dve")
        s_var, s_pow = sem("s_var"), sem("s_pow")
        s_xr, s_rt, s_rte, s_lg = sem("s_xr"), sem("s_rt"), sem("s_rte"), sem("s_lg")
        s_shift, s_exp = sem("s_shift"), sem("s_exp")
        s_rowsum, s_count = sem("s_rowsum"), sem("s_count")
        s_slot, s_rows = sem("s_slot"), sem("s_rows")
        s_scat = [sem(f"s_scat{h}") for h in range(HALVES)]
        s_xe = [sem(f"s_xe{r}") for r in range(RING)]
        s_xt, s_xte, s_u1, s_u3 = sem("s_xt"), sem("s_xte"), sem("s_u1"), sem("s_u3")
        s_act, s_hid, s_ht, s_hte = sem("s_act"), sem("s_hid"), sem("s_ht"), sem("s_hte")
        s_y, s_ye = sem("s_y"), sem("s_ye")
        s_st = [sem(f"s_st{r}") for r in range(RING)]
        GC = 4
        s_gath = [[sem(f"s_gath{h}_{c}") for c in range(GC)] for h in range(HALVES)]
        s_comb = sem("s_comb")
        s_out = sem("s_out")
        s_xa, s_at, s_ate, s_qk, s_v, s_ve = (sem(n) for n in ("s_xa", "s_at", "s_ate", "s_qk", "s_v", "s_ve"))
        s_hi, s_res, s_mid, s_lo, s_wr = (sem(n) for n in ("s_hi", "s_res", "s_mid", "s_lo", "s_wr"))
        s_stack = [[sem(f"s_stack{q}_{c}") for c in range(2)] for q in range(2)]
        s_mrow = [sem(f"s_mrow{q}") for q in range(2)]
        s_s, s_max, s_nm, s_nmt, s_nmte = (sem(n) for n in ("s_s", "s_max", "s_nm", "s_nmt", "s_nmte"))
        s_sc, s_exp2, s_av, s_ove = (sem(n) for n in ("s_sc", "s_exp2", "s_av", "s_ove"))
        s_ot, s_on, s_ont, s_onte, s_proj, s_add = (sem(n) for n in ("s_ot", "s_on", "s_ont", "s_onte",
                                                                     "s_proj", "s_add"))
        s_wa, s_vzero = sem("s_wa"), sem("s_vzero")

        chain = [0]

        def link(eng, ins):
            chain[0] += 1
            ins.then_inc(s_dve, 1)
            eng.wait_ge(s_dve, chain[0])

        block = ctx.enter_context(nc.Block())

        def norm_stats(eng, h):
            xh = X[:, h * TH:(h + 1) * TH, :]

            def stat(i, r, j):
                eng.bn_stats(one(stats6[:, :, :], i), one(xh, i)).then_inc(s_dve, 1)

            steps(eng, 0, TH, 0, TH, stat)
            chain[0] += TH
            eng.wait_ge(s_dve, chain[0])
            link(eng, eng.tensor_tensor(msum[:], stats6[:, :, 1], stats6[:, :, 4], ALU.add))
            link(eng, eng.tensor_tensor(mdiff[:], stats6[:, :, 1], stats6[:, :, 4], ALU.subtract))
            link(eng, eng.tensor_tensor(var[:], stats6[:, :, 2], stats6[:, :, 5], ALU.add))
            link(eng, eng.tensor_scalar(mean[:], msum[:], 0.5, None, ALU.mult))
            link(eng, eng.scalar_tensor_tensor(msq[:], mdiff[:], 0.25, mdiff[:], ALU.mult, ALU.mult))
            link(eng, eng.tensor_scalar(var[:], var[:], 1.0 / D, LN_EPS, ALU.mult, ALU.add))
            eng.tensor_tensor(var[:], var[:], msq[:], ALU.add).then_inc(s_var, 1)

        def norm_root(eng, n):
            eng.wait_ge(s_pow, n + 1)
            link(eng, eng.tensor_tensor(rr[:], rough[:], rough[:], ALU.mult))
            link(eng, eng.scalar_tensor_tensor(rr[:], rr[:], -0.5, var[:], ALU.mult, ALU.mult))
            link(eng, eng.scalar_tensor_tensor(rstd[:], rr[:], 1.5, rough[:], ALU.add, ALU.mult))

        def route_vector(eng, g, n, h):
            xh = X[:, h * TH:(h + 1) * TH, :]
            norm_stats(eng, h)
            norm_root(eng, n)
            b = g * TH

            def normed(i, r, j):
                wait(eng, s_rt, b + i - 1)
                eng.tensor_scalar(xr[:, r, :], one(xh, i), one(mean[:, :].unsqueeze(2), i),
                                  one(rstd[:, :].unsqueeze(2), i), ALU.subtract, ALU.mult).then_inc(s_xr, 1)

            steps(eng, 0, TH, 2, TH, normed)
            eng.wait_ge(s_lg, b + TH)
            logits = PS[2][:, 0:TH * EXPERTS].rearrange("p (t e) -> p t e", e=EXPERTS)
            over_e = lambda a: a.unsqueeze(2).to_broadcast([P, TH, EXPERTS])
            over_t = lambda a: a.unsqueeze(1).to_broadcast([P, TH, EXPERTS])
            rev = over_t(CT[:, C_REV:C_STEP])
            link(eng, eng.tensor_reduce(colmax[:], logits, AX.X, ALU.max))
            eng.tensor_tensor(shifted[:], logits, over_e(colmax[:, :]), ALU.subtract).then_inc(s_shift, 1)
            eng.wait_ge(s_exp, g + 1)
            link(eng, eng.tensor_reduce(total[:], weight[:], AX.X, ALU.add))
            link(eng, eng.reciprocal(total[:], total[:]))
            link(eng, eng.tensor_tensor(score[:], weight[:], over_e(total[:, :]), ALU.mult))
            link(eng, eng.tensor_tensor(biased[:], score[:], over_t(BIAS[:, :]), ALU.add))
            for k in range(TOP_K):
                link(eng, eng.tensor_reduce(colmax[:], biased[:], AX.X, ALU.max))
                link(eng, eng.tensor_tensor(found[:], biased[:], over_e(colmax[:, :]), ALU.is_equal))
                link(eng, eng.tensor_tensor(found[:], found[:], rev, ALU.mult))
                link(eng, eng.tensor_reduce(colmax[:], found[:], AX.X, ALU.max))
                link(eng, eng.tensor_tensor(chosen[:, k], rev, over_e(colmax[:, :]), ALU.is_equal))
                if k + 1 < TOP_K:
                    link(eng, eng.scalar_tensor_tensor(biased[:], chosen[:, k], -FAR, biased[:],
                                                       ALU.mult, ALU.add))
            for k in range(TOP_K):
                link(eng, eng.tensor_tensor(picked[:, k], chosen[:, k], score[:], ALU.mult))
            link(eng, eng.tensor_reduce(coef[:], picked[:], AX.X, ALU.add))
            for k in range(TOP_K):
                link(eng, eng.tensor_tensor(coef[:, k], coef[:, k], rstd[:], ALU.mult))
            link(eng, eng.tensor_tensor(taken[:].rearrange("p e t -> p t e"), chosen[:, 0], chosen[:, 1],
                                        ALU.add))
            eng.tensor_reduce(rowsum[:], taken[:], AX.X, ALU.add).then_inc(s_rowsum, 1)
            flat = lambda a: a[:].rearrange("p e t -> p (e t)")
            link(eng, eng.tensor_tensor_scan(flat(upto), CT[:, C_SEG:C_END], flat(taken), 0.0,
                                             ALU.mult, ALU.add))
            link(eng, eng.tensor_tensor(place[:], upto[:], taken[:], ALU.subtract))

            def scaled(k):
                def body(i, r, j):
                    eng.tensor_scalar(one(rows[h][:, k], i), one(xh, i), one(mean[:, :].unsqueeze(2), i),
                                      one(coef[:, k].unsqueeze(2), i), ALU.subtract, ALU.mult)\
                       .then_inc(s_rows, 1)
                return body

            eng.wait_ge(s_count, g + 1)
            before, counts = PS[3][:, 0:EXPERTS], PS[3][:, EXPERTS:2 * EXPERTS]
            et = [P, EXPERTS, TH]
            link(eng, eng.tensor_tensor(over[:], counts.unsqueeze(2).to_broadcast(et),
                                        CT[:, C_STEP:C_TILE].unsqueeze(1).to_broadcast(et), ALU.is_gt))
            link(eng, eng.tensor_reduce(tiles_of[:], over[:], AX.X, ALU.add))
            link(eng, eng.tensor_tensor_scan(last_tile[:], CT[:, C_ONES:C_ONES + EXPERTS], tiles_of[:],
                                             0.0, ALU.mult, ALU.add))
            link(eng, eng.tensor_tensor(start[:], last_tile[:], tiles_of[:], ALU.subtract))
            link(eng, eng.scalar_tensor_tensor(start[:], start[:], float(P), before, ALU.mult, ALU.add))
            link(eng, eng.tensor_tensor(place[:], place[:], start[:, :].unsqueeze(2).to_broadcast(et), ALU.add))
            for k in range(TOP_K):
                link(eng, eng.tensor_tensor(picked[:, k], chosen[:, k],
                                            place[:].rearrange("p e t -> p t e"), ALU.mult))
            link(eng, eng.tensor_reduce(slot_f[:], picked[:], AX.X, ALU.add))
            eng.tensor_copy(slot[h][:], slot_f[:]).then_inc(s_slot, 1)
            ne = [P, NT, EXPERTS]
            link(eng, eng.tensor_tensor(passed[:], CT[:, C_TILE:C_SEG].unsqueeze(2).to_broadcast(ne),
                                        last_tile[:, :].unsqueeze(1).to_broadcast(ne), ALU.is_ge))
            link(eng, eng.tensor_reduce(expert_f[:], passed[:], AX.X, ALU.add))
            link(eng, eng.tensor_scalar(expert_f[:], expert_f[:], float(EXPERTS - 1), None, ALU.min))
            eng.tensor_copy(expert[h][:], expert_f[:]).then_inc(s_slot, 1)
            for k in range(TOP_K):
                steps(eng, 0, TH, 0, TH, scaled(k))

        def route_tensor(eng, g):
            b = g * TH

            def turn(i, r):
                eng.wait_ge(s_xr, b + i + 1)
                wait(eng, s_rte, b + i - 1)
                eng.transpose(PS[r][:, 0:P], xr[:, r, :], ident).then_inc(s_rt, 1)

            wait(eng, s_shift, g)

            def logits(i, r):
                eng.wait_ge(s_rte, b + i + 1)
                eng.matmul(PS[2][:, bass.ds(i * EXPERTS, EXPERTS)], xrT[:, r, :], GATE[:],
                           start=True, stop=True).then_inc(s_lg, 1)

            def body(i, r, j):
                if not (isinstance(i, int) and i >= TH):
                    turn(i, r)
                if not (isinstance(i, int) and i == 0):
                    logits(i - 1, 1 - r)

            steps(eng, 0, TH + 1, 2, TH, body)
            eng.wait_ge(s_rowsum, g + 1)
            eng.matmul(PS[3][:, 0:EXPERTS], CT[:, C_BEFORE:C_BEFORE + P], rowsum[:], start=True, stop=True)
            eng.matmul(PS[3][:, EXPERTS:2 * EXPERTS], ones, rowsum[:], start=True, stop=True)\
               .then_inc(s_count, 1)

        def route_scalar(eng, g):
            b = g * TH

            def body(i, r, j):
                eng.wait_ge(s_rt, b + i + 1)
                wait(eng, s_lg, b + i - 1)
                eng.copy(xrT[:, r, :], PS[r][:, 0:P]).then_inc(s_rte, 1)

            steps(eng, 0, TH, 2, TH, body)
            eng.wait_ge(s_shift, g + 1)
            eng.activation(weight[:], shifted[:], ACT.Exp).then_inc(s_exp, 1)

        def root_gpsimd(eng, n):
            eng.wait_ge(s_var, n + 1)
            eng.tensor_tensor(rough[:], var[:], half_power[:], ALU.pow).then_inc(s_pow, 1)

        def scatter_gpsimd(eng, g, h):
            if g < HALVES:
                eng.wait_ge(s_cleared[h], 16)
            eng.wait_ge(s_slot, 2 * (g + 1))
            for k in range(TOP_K):
                for t in range(TH):
                    if t % 4 == 0:
                        eng.wait_ge(s_rows, (TOP_K * g + k) * TH + t + 4)
                    eng.indirect_dma_start(slots_in[h], bass.IndirectOffsetOnAxis(ap=slot[h][:, k, t:t + 1], axis=0),
                                           rows[h][:, k, t, :], None).then_inc(s_scat[h], 16)

        def gather_gpsimd(eng, g, h):
            for r in range(RING):
                eng.wait_ge(s_st[r], 16 * stored(g + 1, r))
            per = TH // GC
            for c in range(GC):
                for t in range(c * per, (c + 1) * per):
                    for k in range(TOP_K):
                        eng.indirect_dma_start(rows[h][:, k, t, :], None, slots_out[h],
                                               bass.IndirectOffsetOnAxis(ap=slot[h][:, k, t:t + 1], axis=0))\
                           .then_inc(s_gath[h][c], 16)

        def combine_vector(eng, g, h):
            per = TH // GC
            for c in range(GC):
                eng.wait_ge(s_gath[h][c], 16 * TOP_K * per * (g // HALVES + 1))
                a, b = (rows[h][:, k, c * per:(c + 1) * per, :] for k in range(TOP_K))
                xc = X[:, h * TH + c * per:h * TH + (c + 1) * per, :]
                link(eng, eng.tensor_tensor(a, a, b, ALU.add))
                link(eng, eng.scalar_tensor_tensor(xc, a, 0.5, xc, ALU.mult, ALU.add))

        def stored(g, r):
            return g * len(range(r, NT, RING))

        def expert_sync(eng, g, h):
            b = g * NT
            eng.wait_ge(s_scat[h], 16 * TOP_K * TH * (g // HALVES + 1))
            lag = RING + 2

            def body(i, r, j):
                fixed = isinstance(i, int)
                if not fixed or i < NT:
                    wait(eng, s_xt, b + i - RING + 1)
                    eng.dma_start(xe[:, r, :], slots_in[h][bass.ds(i * P, P), :]).then_inc(s_xe[r], 16)
                if not fixed or i >= lag:
                    eng.wait_ge(s_ye, b + i - lag + 1)
                    q = (r - lag) % RING
                    eng.dma_start(slots_out[h][bass.ds((i - lag) * P, P), :], ye[:, q, :]).then_inc(s_st[q], 16)

            steps(eng, 0, NT + lag, 2 * RING, NT, body, RING)

        def expert_tensor(eng, g, h, routed):
            b = g * NT

            def number(i):
                return eng.value_load(expert[h][0:1, bass.ds(i, 1)], min_val=0, max_val=EXPERTS - 1)

            def turn(i, r, j):
                eng.wait_ge(s_xe[r], 16 * (stored(g, r) + 1 + j))
                wait(eng, s_xte, b + i)
                eng.transpose(PS[0][:, 0:P], xe[:, r, :], ident).then_inc(s_xt, 1)

            def up(i, r):
                e = number(i)
                eng.wait_ge(s_xte, b + i + 1)
                wait(eng, s_act, b + i - 1)
                eng.matmul(PS[2 + r][:, 0:HIDDEN], xeT[:, r, :], one(W1[:, :, :], e), start=True, stop=True)\
                   .then_inc(s_u1, 1)
                wait(eng, s_hid, b + i - 1)
                eng.matmul(PS[4 + r][:, 0:HIDDEN], xeT[:, r, :], one(W3[:, :, :], e), start=True, stop=True)\
                   .then_inc(s_u3, 1)

            def down(i, r):
                e = number(i)
                eng.wait_ge(s_hte, b + i + 1)
                wait(eng, s_ye, b + i)
                for c in range(HC):
                    last = eng.matmul(PS[1][:, 0:D], hidT[:, r, c * P:(c + 1) * P], one(W2[:, :, c, :], e),
                                      start=c == 0, stop=c == HC - 1)
                last.then_inc(s_y, 1)

            def turn_hidden(i, r):
                eng.wait_ge(s_hid, b + i + 1)
                wait(eng, s_hte, b + i - 1)
                for c in range(HC):
                    last = eng.transpose(PS[6 + r][:, c * P:(c + 1) * P], hid[:, r, c * P:(c + 1) * P], ident)
                last.then_inc(s_ht, 1)

            def body(i, r, j):
                fixed = isinstance(i, int)
                if not fixed or -1 <= i < NT - 1:
                    turn(i + 1, (r + 1) % RING, j + (r + 1) // RING)
                if not fixed or 0 <= i < NT:
                    up(i, r % 2)
                if not fixed or 2 <= i:
                    down(i - 2, r % 2)
                if not fixed or 1 <= i <= NT:
                    turn_hidden(i - 1, 1 - r % 2)

            if g == 0:
                eng.wait_ge(s_w, 16 * (3 + EXPERTS))
            eng.wait_ge(s_slot, 2 * routed)
            steps(eng, -1, NT + 2, RING, NT - 1, body, RING)

        def expert_scalar(eng, g):
            b = g * NT

            def body(i, r, j):
                fixed = isinstance(i, int)
                if not fixed or -1 <= i < NT - 1:
                    eng.wait_ge(s_xt, b + i + 2)
                    wait(eng, s_u3, b + i)
                    eng.copy(xeT[:, 1 - r % 2, :], PS[0][:, 0:P]).then_inc(s_xte, 1)
                if not fixed or 0 <= i < NT:
                    eng.wait_ge(s_u1, b + i + 1)
                    wait(eng, s_hid, b + i - 1)
                    eng.activation(act1[:, r % 2, :], PS[2 + r % 2][:, 0:HIDDEN], ACT.Silu).then_inc(s_act, 1)
                if not fixed or 2 <= i:
                    q, before = (r - 2) % RING, j + (r - 2) // RING
                    eng.wait_ge(s_y, b + i - 1)
                    wait(eng, s_st[q], 16 * (stored(g, q) + before))
                    eng.copy(ye[:, q, :], PS[1][:, 0:D]).then_inc(s_ye, 1)

            steps(eng, -1, NT + 2, RING, NT - 1, body, RING)

        def expert_vector(eng, g):
            b = g * NT

            def body(i, r, j):
                fixed = isinstance(i, int)
                if not fixed or i < NT:
                    eng.wait_ge(s_act, b + i + 1)
                    eng.wait_ge(s_u3, b + i + 1)
                    wait(eng, s_ht, b + i - 1)
                    eng.tensor_tensor(hid[:, r % 2, 0:HIDDEN], PS[4 + r % 2][:, 0:HIDDEN], act1[:, r % 2, :], ALU.mult)\
                       .then_inc(s_hid, 1)
                if not fixed or i >= 1:
                    eng.wait_ge(s_ht, b + i)
                    wait(eng, s_y, b + i - 2)
                    eng.tensor_copy(hidT[:, 1 - r % 2, :], PS[7 - r % 2][:, 0:HP]).then_inc(s_hte, 1)

            steps(eng, 0, NT + 1, RING, NT - 1, body, RING)

        FILLS = ((0, 3), (3, 6), (6, 9), (9, 12), (12, 14), (14, 16), (16, 16), (16, 16))
        scale = float(HD) ** -0.5

        def fills(u):
            return [(f, f // 2, f % 2) for f in range(*FILLS[u])]

        def attention_tensor(eng, h):
            for b in range(-2, NB + 1):
                n = h * NB + b
                ahead, nxt, now, done = (0 <= b + 2 < NB, 0 <= b + 1 < NB, 0 <= b < NB, 0 <= b - 1 < NB)
                for u in range(PAIRS):
                    if now:
                        q = n % 2
                        if u == 0:
                            eng.wait_ge(s_mrow[q], 64 * (n // 2 + 1))
                        wait(eng, s_exp2, PAIRS * n + u - 1)
                        for kt in range(2):
                            last = eng.matmul(PS[2 * (u % 2) + kt], KS[q][:, u, kt * P:(kt + 1) * P],
                                              QS[q][:, u, :, :].rearrange("p e n -> p (e n)"),
                                              start=True, stop=True)
                        last.then_inc(s_sc, 1)
                    if nxt:
                        m, q = n + 1, (n + 1) % 2
                        for f, pair, qt in fills(u):
                            if f % 8 == 0:
                                eng.wait_ge(s_stack[q][f // 8], 80 * (m // 2 + 1))
                            wait(eng, s_max, 2 * PAIRS * m + f - 1)
                            for e in range(2):
                                last = eng.matmul(PS[4 + f % 2][:, e * SEQ:(e + 1) * SEQ],
                                                  QS[q][:, pair, e, qt * P:(qt + 1) * P], KS[q][:, pair, :],
                                                  start=True, stop=True)
                            last.then_inc(s_s, 1)
                    if now and u > 0:
                        values(eng, n, u - 1)
                    if ahead and u == 0:
                        m = n + 2
                        eng.wait_ge(s_xa, 2 * (m + 1))
                        wait(eng, s_ve, m)
                        wait(eng, s_nmte, n + 1 if b >= 0 else h * NB)
                        wait(eng, s_add, max(h * NB, n - 1))
                        for i in range(2):
                            last = eng.transpose(PS[7][:, i * P:(i + 1) * P], xa[:, i, :], ident)
                        last.then_inc(s_at, 1)
                    if ahead and u == 1:
                        eng.wait_ge(s_ate, n + 3)
                        for side, w in enumerate((WQ, WK)):
                            last = eng.matmul(PS[7][:, side * SEQ:(side + 1) * SEQ], w[:], xaT[:],
                                              start=True, stop=True)
                        last.then_inc(s_qk, 1)
                    if ahead and u == 2:
                        eng.wait_ge(s_res, n + 3)
                        for kt in range(2):
                            last = eng.matmul(PS[7][:, kt * P:(kt + 1) * P], xaT[:, kt * P:(kt + 1) * P], WV[:],
                                              start=True, stop=True)
                        last.then_inc(s_v, 1)
                    if done and u in (3, 4):
                        qt = u - 3
                        eng.wait_ge(s_ove, 2 * n)
                        if u == 3:
                            eng.wait_ge(s_ve, min(n + 3, (h + 1) * NB))
                            eng.wait_ge(s_nmte, min(n + 1, (h + 1) * NB))
                            wait(eng, s_add, n - 1)
                        else:
                            eng.wait_ge(s_on, 2 * n - 1)
                        for c in range(HEADS // 4):
                            last = eng.transpose(PS[7][:, c * P:(c + 1) * P], oT[:, c, qt * P:(qt + 1) * P], ident)
                        last.then_inc(s_ot, 1)
                    if done and u == 5:
                        eng.wait_ge(s_on, 2 * n)
                        for qt in range(2):
                            last = eng.transpose(PS[7][:, qt * P:(qt + 1) * P], on[:, qt, :], ident)
                        last.then_inc(s_ont, 1)
                    if nxt and u == 6:
                        eng.wait_ge(s_nm, n + 2)
                        if done:
                            eng.wait_ge(s_onte, n)
                        elif ahead:
                            eng.wait_ge(s_ve, n + 3)
                        for qt in range(2):
                            last = eng.transpose(PS[7][0:4 * PAIRS, :].bitcast(BF16)[:, qt * P:(qt + 1) * P],
                                                 nm[:, qt, :], identb[:])
                        last.then_inc(s_nmt, 1)
                    if done and u == 7:
                        eng.wait_ge(s_onte, n)
                        if nxt:
                            eng.wait_ge(s_nmte, n + 2)
                        for qt in range(2):
                            last = eng.matmul(PS[7][:, qt * P:(qt + 1) * P], onT[:, qt * P:(qt + 1) * P], WO[:],
                                              start=True, stop=True)
                        last.then_inc(s_proj, 1)
                if now:
                    values(eng, n, PAIRS - 1)

        def values(eng, n, u):
            eng.wait_ge(s_exp2, PAIRS * n + u + 1)
            if u == 0:
                eng.wait_ge(s_ve, n + 1)
            if u % 4 == 0:
                wait(eng, s_ove, 2 * n + u // 4)
            for e in range(2):
                j = (2 * u + e) % 4
                for kt in range(2):
                    last = eng.matmul(PS[6][32 * j:32 * j + 32, (u // 2 % 2) * SEQ:(u // 2 % 2 + 1) * SEQ],
                                      V1[n % 3][:, kt, 2 * u + e, :], PT[:, u % 2, kt, e, :],
                                      start=kt == 0, stop=kt == 1, tile_position=(0, 32 * j))
            last.then_inc(s_av, 1)

        def attention_scalar(eng, h):
            for b in range(-2, NB + 1):
                n = h * NB + b
                ahead, nxt, now, done = (0 <= b + 2 < NB, 0 <= b + 1 < NB, 0 <= b < NB, 0 <= b - 1 < NB)
                for u in range(PAIRS):
                    if now:
                        eng.wait_ge(s_sc, PAIRS * n + u + 1)
                        wait(eng, s_av, PAIRS * n + u - 1)
                        eng.activation(PT[:, u % 2].rearrange("p k e n -> p (k e n)"), ST[u % 2], ACT.Exp,
                                       scale=scale).then_inc(s_exp2, 1)
                    if u == 0 and done:
                        read_values(eng, n - 1, 1)
                    if u == 4 and now:
                        read_values(eng, n, 0)
                    if u == 0 and ahead:
                        eng.wait_ge(s_at, n + 3)
                        wait(eng, s_v, n + 2)
                        eng.copy(xaT[:], PS[7][:, 0:SEQ]).then_inc(s_ate, 1)
                    if u == 1 and ahead:
                        eng.wait_ge(s_qk, n + 3)
                        wait(eng, s_wr, 112 * (n + 2))
                        eng.copy(split[:, :, 0, :], PS[7][:, :].rearrange("p (s n) -> p s n", s=2)).then_inc(s_hi, 1)
                        eng.wait_ge(s_res, n + 3)
                        eng.copy(split[:, :, 1, :], resid[:, :, :]).then_inc(s_mid, 1)
                    if u == 2 and ahead:
                        q = (n + 2) % 3
                        eng.wait_ge(s_v, n + 3)
                        wait(eng, s_av, PAIRS * n)
                        eng.copy(V1[q][:, :, :, 0:HD],
                                 PS[7][:, 0:2 * P].rearrange("p (k a d) -> p k a d", k=2, d=HD)).then_inc(s_ve, 1)
                    if u == 5 and done:
                        eng.wait_ge(s_ont, n)
                        wait(eng, s_proj, n - 1)
                        eng.copy(onT[:], PS[7][:, 0:SEQ]).then_inc(s_onte, 1)
                    if u == 6 and nxt:
                        eng.wait_ge(s_nmt, n + 2)
                        if n + 1 > 0:
                            p = n % 2
                            eng.wait_ge(s_mrow[p], 64 * (n // 2 + 1))
                        eng.copy(nmT[:], PS[7][0:4 * PAIRS, :].bitcast(BF16)[:, 0:SEQ]).then_inc(s_nmte, 1)

        def read_values(eng, n, i):
            eng.wait_ge(s_av, PAIRS * n + 4 * (i + 1))
            wait(eng, s_ot, 2 * n)
            eng.copy(oT[:, 2 * i:2 * i + 2, :].rearrange("p c n -> p (c n)"), PS[6][:, :]).then_inc(s_ove, 1)

        def normed_pair(eng, h, b):
            n = h * NB + b
            wait(eng, s_at, n)
            for i in range(2):
                t = 2 * b + i
                eng.tensor_scalar(xa[:, i, :], X[:, h * TH + t, :], mean[:, t:t + 1], rstd[:, t:t + 1],
                                  ALU.subtract, ALU.mult).then_inc(s_xa, 1)

        def attention_vector(eng, h, norm):
            norm_stats(eng, h)
            norm_root(eng, norm)
            normed_pair(eng, h, 0)
            for b in range(-2, NB + 1):
                n = h * NB + b
                ahead, nxt, now, done = (0 <= b + 2 < NB, 0 <= b + 1 < NB, 0 <= b < NB, 0 <= b - 1 < NB)
                for u in range(PAIRS):
                    if nxt:
                        for f, pair, qt in fills(u):
                            eng.wait_ge(s_s, 2 * PAIRS * (n + 1) + f + 1)
                            eng.tensor_reduce(mx[:, qt, :, pair], PS[4 + f % 2][:, :].rearrange("p (e n) -> p e n", e=2),
                                              AX.X, ALU.max).then_inc(s_max, 1)
                    if u == 1 and ahead:
                        eng.wait_ge(s_hi, n + 3)
                        eng.tensor_tensor(resid[:], PS[7][:, :].rearrange("p (s n) -> p s n", s=2),
                                          split[:, :, 0, :], ALU.subtract).then_inc(s_res, 1)
                        eng.wait_ge(s_mid, n + 3)
                        eng.tensor_tensor(split[:, :, 2, :], resid[:], split[:, :, 1, :], ALU.subtract).then_inc(s_lo, 1)
                    if u in (3, 4) and done:
                        qt = u - 3
                        eng.wait_ge(s_ot, 2 * n - 1 + qt)
                        sums = PS[7][:, :].rearrange("p (a c) -> p a c", c=32)
                        link(eng, eng.reciprocal(rsum[:, qt, :], sums[:, :, HD]))
                        wait(eng, s_ont, n - 1)
                        eng.tensor_tensor(on[:, qt, :].rearrange("p (a d) -> p a d", d=HD), sums[:, :, 0:HD],
                                          rsum[:, qt, :].unsqueeze(2).to_broadcast([P, HEADS, HD]),
                                          ALU.mult).then_inc(s_on, 1)
                    if u == 5 and nxt:
                        eng.wait_ge(s_max, 2 * PAIRS * (n + 2))
                        wait(eng, s_nmt, n + 1)
                        m4 = mx[:].rearrange("p q e r -> p (q e) r")
                        n4 = nm[:].rearrange("p q (e t r) -> p (q e) t r", e=2, t=2)
                        link(eng, eng.tensor_scalar(n4[:, :, 0, :], m4, -1.0, None, ALU.mult))
                        eng.scalar_tensor_tensor(n4[:, :, 1, :], m4, -1.0, n4[:, :, 0, :], ALU.mult,
                                                 ALU.subtract).then_inc(s_nm, 1)
                    if u == 6 and 0 <= b + 3 < NB:
                        normed_pair(eng, h, b + 3)
                    if u == 7 and done:
                        eng.wait_ge(s_proj, n)
                        xb = X[:, h * TH + 2 * (b - 1):h * TH + 2 * b, :]
                        eng.tensor_tensor(xb, PS[7][:, 0:SEQ].rearrange("p (q n) -> p q n", q=2), xb,
                                          ALU.add).then_inc(s_add, 1)

        def attention_sync(eng, h):
            for b in range(-2, NB):
                n = h * NB + b
                if 0 <= b + 2 < NB:
                    m, q = n + 2, n % 2
                    eng.wait_ge(s_lo, m + 1)
                    if m >= 2:
                        for c in range(2):
                            eng.wait_ge(s_stack[q][c], 80 * (m // 2))
                    flat = scratch[q].rearrange("s e r d t n -> s (e r d) t n")
                    eng.dma_start(flat[0, :, 0:3, :], split[:, 0, :, :]).then_inc(s_wr, 16)
                    eng.dma_start(flat[1, :, 0:2, :], split[:, 1, 0:2, :]).then_inc(s_wr, 16)
                    eng.dma_start(flat[0, :, 3:5, :], split[:, 0, 0:2, :]).then_inc(s_wr, 16)
                    eng.dma_start(flat[1, :, 2:4, :], split[:, 1, 0:2, :]).then_inc(s_wr, 16)
                    eng.dma_start(flat[0, :, 5, :], split[:, 0, 0, :]).then_inc(s_wr, 16)
                    eng.dma_start(flat[1, :, 4, :], split[:, 1, 0, :]).then_inc(s_wr, 16)
                    eng.dma_start(flat[1, :, 5, :], split[:, 1, 2, :]).then_inc(s_wr, 16)
                    eng.wait_ge(s_wr, 112 * (m + 1))
                    stack(eng, n, m, 0)
                if 0 <= b + 1 < NB:
                    m, q = n + 1, (n + 1) % 2
                    eng.wait_ge(s_nmte, m + 1)
                    for e in range(2):
                        for t in range(2):
                            row = STACK + 2 * e + t
                            first = (2 * e + t) * PAIRS
                            eng.dma_start(QS[q][row:row + 1, :, e, :], nmT[first:first + PAIRS, :])\
                               .then_inc(s_mrow[q], 16)
                if 0 <= b + 2 < NB:
                    stack(eng, n, n + 2, 1)

        def stack(eng, n, m, c):
            q = m % 2
            wait(eng, s_sc, PAIRS * n + 4 * (c + 1))
            pairs = slice(4 * c, 4 * c + 4)
            for e in range(2):
                for side, dst in ((0, QS[q][:, pairs, e, :]), (1, KS[q][:, pairs, :])):
                    eng.dma_start(dst[e * STACK // 2:(e + 1) * STACK // 2],
                                  scratch[q, side, e, pairs].rearrange("r d t n -> (d t) r n"))\
                       .then_inc(s_stack[q][c], 16)
            eng.dma_start(QS[q][STACK:STACK + 4, pairs, :, :].rearrange("p r e n -> p (r e n)"), zrows[:])\
               .then_inc(s_stack[q][c], 16)


        @block.sync
        def _(sp):
            xv = x.rearrange("(t p) d -> p t d", p=P)
            sp.dma_start(CT[:], consts).then_inc(s_const, 16)
            sp.dma_start(X[:, 0:TH, :], xv[:, 0:TH, :]).then_inc(s_x[0], 16)
            sp.dma_start(GATE[:], gate).then_inc(s_const, 16)
            sp.dma_start(BIAS[:], bias.partition_broadcast(P)).then_inc(s_const, 16)
            sp.dma_start(X[:, TH:TILES, :], xv[:, TH:TILES, :]).then_inc(s_x[1], 16)
            sp.wait_ge(s_zero, 1)
            for h in range(HALVES):
                sp.dma_start(slots_in[h].rearrange("(p r) d -> p (r d)", p=P).rearrange("p (a n) -> p a n", a=4),
                             zeros[:, :].unsqueeze(1).to_broadcast([P, 4, NT * 32])).then_inc(s_cleared[h], 16)
            sp.dma_start(W1[:], w1.rearrange("e d h -> d e h")).then_inc(s_w, 16)
            sp.dma_start(W3[:], w3.rearrange("e d h -> d e h")).then_inc(s_w, 16)
            full = HIDDEN // P * P
            for e in range(EXPERTS):
                sp.dma_start(W2[:, e, 0:HC - 1, :], w2[e, 0:full, :].rearrange("(c p) d -> p c d", p=P))\
                  .then_inc(s_w, 16)
            sp.wait_ge(s_zero, 4)
            sp.dma_start(W2[0:HIDDEN - full, :, HC - 1, :], w2[:, full:HIDDEN, :].rearrange("e p d -> p e d"))\
              .then_inc(s_w, 16)
            for w, a in ((WQ, wq), (WK, wk), (WV, wv), (WO, wo)):
                sp.dma_start(w[:], a).then_inc(s_wa, 16)
            ov = out.rearrange("(t p) d -> p t d", p=P)
            if stop != "attn":
                expert_sync(sp, 0, 0)
                expert_sync(sp, 1, 1)
            if stop != "ffn":
                attention_sync(sp, 0)
                attention_sync(sp, 1)
            if not stop:
                expert_sync(sp, 2, 0)
                expert_sync(sp, 3, 1)
            for h in range(HALVES):
                sp.wait_ge(s_comb, h + 1)
                sp.dma_start(ov[:, h * TH:(h + 1) * TH, :], X[:, h * TH:(h + 1) * TH, :]).then_inc(s_out, 16)
            sp.wait_ge(s_out, 16 * HALVES)

        @block.gpsimd
        def _(pool):
            pool.memset(zeros[:], 0.0).then_inc(s_zero, 1)
            pool.memset(half_power[:], -0.5).then_inc(s_zero, 1)
            pool.memset(hid[:, :, HIDDEN:HP], 0.0).then_inc(s_zero, 1)
            pool.wait_ge(s_zero, 3)
            pool.memset(W2[HIDDEN % P:P, :, HC - 1, :], 0.0).then_inc(s_zero, 1)
            pool.wait_ge(s_zero, 4)
            if stop != "attn":
                root_gpsimd(pool, 0)
                root_gpsimd(pool, 1)
                scatter_gpsimd(pool, 0, 0)
                scatter_gpsimd(pool, 1, 1)
                gather_gpsimd(pool, 0, 0)
                gather_gpsimd(pool, 1, 1)
            if not stop:
                root_gpsimd(pool, 2)
                root_gpsimd(pool, 3)
                scatter_gpsimd(pool, 2, 0)
                root_gpsimd(pool, 4)
                root_gpsimd(pool, 5)
                scatter_gpsimd(pool, 3, 1)
                gather_gpsimd(pool, 2, 0)
                gather_gpsimd(pool, 3, 1)
            if stop == "attn":
                root_gpsimd(pool, 0)
                root_gpsimd(pool, 1)

        @block.scalar
        def _(act):
            if stop != "attn":
                route_scalar(act, 0)
                route_scalar(act, 1)
                expert_scalar(act, 0)
                expert_scalar(act, 1)
            if stop == "attn":
                attention_scalar(act, 0)
                attention_scalar(act, 1)
            if not stop:
                attention_scalar(act, 0)
                route_scalar(act, 2)
                attention_scalar(act, 1)
                route_scalar(act, 3)
                expert_scalar(act, 2)
                expert_scalar(act, 3)

        @block.tensor
        def _(pe):
            pe.wait_ge(s_const, 48)
            if stop != "attn":
                route_tensor(pe, 0)
                route_tensor(pe, 1)
                pe.wait_ge(s_zero, 4)
                expert_tensor(pe, 0, 0, 2)
                expert_tensor(pe, 1, 1, 2)
                pe.wait_ge(s_ye, 2 * NT)
                pe.wait_ge(s_hte, 2 * NT)
            pe.wait_ge(s_wa, 64)
            pe.wait_ge(s_vzero, 8)
            if stop == "attn":
                attention_tensor(pe, 0)
                attention_tensor(pe, 1)
            if not stop:
                attention_tensor(pe, 0)
                pe.wait_ge(s_exp2, PAIRS * NB)
                route_tensor(pe, 2)
                pe.wait_ge(s_slot, 2 * 3)
                attention_tensor(pe, 1)
                pe.wait_ge(s_exp2, 2 * PAIRS * NB)
                pe.wait_ge(s_add, 2 * NB)
                pe.wait_ge(s_ove, 4 * NB)
                route_tensor(pe, 3)
                expert_tensor(pe, 2, 0, 4)
                expert_tensor(pe, 3, 1, 4)

        @block.vector
        def _(dve):
            for q in range(2):
                dve.memset(QS[q][:].rearrange("p r e n -> p (r e n)").bitcast(F32), 0.0).then_inc(s_vzero, 1)
                dve.memset(KS[q][STACK:P], 1.0).then_inc(s_vzero, 1)
            for q in range(3):
                dve.memset(V1[q][:, :, :, HD:32], 0.0).then_inc(s_vzero, 1)
            dve.memset(zrows[:], 0.0).then_inc(s_vzero, 1)
            dve.wait_ge(s_vzero, 8)
            for q in range(3):
                link(dve, dve.memset(V1[q][:, :, :, HD:HD + 1], 1.0))
            dve.wait_ge(s_const, 48)
            link(dve, dve.tensor_copy(identb[:], ident))
            if stop != "attn":
                for h in range(HALVES):
                    dve.wait_ge(s_x[h], 16)
                    route_vector(dve, h, h, h)
                expert_vector(dve, 0)
                expert_vector(dve, 1)
                combine_vector(dve, 0, 0)
            if not stop:
                attention_vector(dve, 0, 2)
                combine_vector(dve, 1, 1)
                dve.wait_ge(s_add, NB)
                route_vector(dve, 2, 3, 0)
                attention_vector(dve, 1, 4)
                dve.wait_ge(s_add, 2 * NB)
                route_vector(dve, 3, 5, 1)
                expert_vector(dve, 2)
                expert_vector(dve, 3)
                for h in range(HALVES):
                    combine_vector(dve, 2 + h, h)
                    dve.memset(colmax[:], 0.0).then_inc(s_comb, 1)
            if stop == "ffn":
                combine_vector(dve, 1, 1)
                dve.memset(colmax[:], 0.0).then_inc(s_comb, 2)
            if stop == "attn":
                dve.wait_ge(s_x[0], 16)
                attention_vector(dve, 0, 0)
                dve.wait_ge(s_x[1], 16)
                attention_vector(dve, 1, 1)
                dve.wait_ge(s_add, 2 * NB)
                dve.memset(colmax[:], 0.0).then_inc(s_comb, 2)


def kernel(L0_attn_hidden_states, L0_attn_Wq, L0_attn_Wk, L0_attn_Wv, L0_attn_Wo, L0_ffn_gate_w,
           L0_ffn_expert_bias, L0_ffn_w1, L0_ffn_w2, L0_ffn_w3):
    import concourse.bacc as bacc
    from concourse.bass_utils import run_bass_kernel_spmd

    def turned(w):
        return np.ascontiguousarray(np.asarray(w).T)

    def by_parity(w):
        w = np.asarray(w).reshape(PAIRS, 2, HD, D)
        return np.ascontiguousarray(w.transpose(3, 1, 0, 2).reshape(D, D))

    arrays = {
        "x": np.ascontiguousarray(L0_attn_hidden_states).reshape(BATCH * SEQ, D),
        "wq": by_parity(L0_attn_Wq), "wk": by_parity(L0_attn_Wk),
        "wv": turned(L0_attn_Wv), "wo": turned(L0_attn_Wo),
        "gate": turned(L0_ffn_gate_w), "bias": np.ascontiguousarray(L0_ffn_expert_bias),
        "w1": np.ascontiguousarray(L0_ffn_w1), "w2": np.ascontiguousarray(L0_ffn_w2),
        "w3": np.ascontiguousarray(L0_ffn_w3), "consts": constants(),
    }
    nc = bacc.Bacc("TRN2", target_bir_lowering=False, num_devices=1)
    aps = {n: nc.dram_tensor(f"in_{n}", a.shape, mybir.dt.from_np(a.dtype), kind="ExternalInput").ap()
           for n, a in arrays.items()}
    out = nc.dram_tensor("out_0", [BATCH * SEQ, D], F32, kind="ExternalOutput").ap()
    build(nc, *aps.values(), out)
    r = run_bass_kernel_spmd(nc, [{f"in_{n}": a for n, a in arrays.items()}], core_ids=[0])
    return r.results[0]["out_0"].reshape(BATCH, SEQ, D)
```

```python
from contextlib import ExitStack

import concourse.bass as bass
import numpy as np
from concourse import mybir

P = 128
BATCH, SEQ, D = 16, 256, 128
HEADS, HD = 16, 8
PAIRS = HEADS // 2
EXPERTS, HIDDEN, TOP_K = 8, 352, 2
TILES = BATCH * SEQ // P
HALVES = 2
TH = TILES // HALVES
NB = BATCH // HALVES
NT = TOP_K * TH + EXPERTS - 1
HC = -(-HIDDEN // P)
HP = HC * P
LN_EPS = 1e-5
FAR = 1e30
SIDE = PAIRS * (NB + 1 - 3)

LOOPS = False
RG = TH // 4
RING = 4
NTERM = 7
STACK = 2 * HD * NTERM

F32, BF16, I32 = mybir.dt.float32, mybir.dt.bfloat16, mybir.dt.int32
ALU, ACT, AX = mybir.AluOpType, mybir.ActivationFunctionType, mybir.AxisListType

C_ID, C_BEFORE, C_ONES = 0, P, 2 * P
C_REV = 3 * P
C_STEP = C_REV + EXPERTS
C_TILE = C_STEP + TH
C_SEG = C_TILE + NT
C_END = C_SEG + EXPERTS * TH


def constants():
    c = np.zeros((P, C_END), np.float32)
    c[:, C_ID:C_ID + P] = np.eye(P)
    c[:, C_BEFORE:C_BEFORE + P] = np.triu(np.ones((P, P)), 1)
    c[:, C_ONES:C_ONES + P] = 1
    c[:, C_REV:C_STEP] = EXPERTS - np.arange(EXPERTS)
    c[:, C_STEP:C_TILE] = P * np.arange(TH)
    c[:, C_TILE:C_SEG] = np.arange(NT)
    c[:, C_SEG:] = np.tile(np.arange(TH) > 0, EXPERTS)
    return c


def wait(eng, sem, value):
    if not isinstance(value, int) or value > 0:
        eng.wait_ge(sem, value)


def steps(eng, first, last, low, high, body, unroll=2):
    high = low + (high - low) // unroll * unroll
    for i in range(first, low):
        body(i, i % unroll, i // unroll)
    if LOOPS:
        with eng.Fori(low // unroll, high // unroll) as j:
            for r in range(unroll):
                body(unroll * j + r, r, j)
    else:
        high = low
    for i in range(high, last):
        body(i, i % unroll, i // unroll)


def advance(side, ticks, i):
    for _ in range(ticks(i)):
        next(side, None)


def at(view, i):
    return view[:, bass.ds(i, 1)]


def one(view, i):
    return at(view, i).squeeze(1)


def build(nc, x, wq, wk, wv, wo, gate, bias, w1, w2, w3, consts, out):
    with ExitStack() as ctx:
        def sb(name, shape, dt=F32):
            return ctx.enter_context(nc.sbuf_tensor(name, shape, dt))

        def sem(name):
            return ctx.enter_context(nc.semaphore(name))

        X = sb("X", [P, TILES, D])
        CT = sb("CT", [P, C_END])
        W1 = sb("W1", [P, EXPERTS, HIDDEN])
        W3 = sb("W3", [P, EXPERTS, HIDDEN])
        W2 = sb("W2", [P, EXPERTS, HC, D])
        GATE = sb("GATE", [P, EXPERTS])
        BIAS = sb("BIAS", [P, EXPERTS])
        ident = CT[:, C_ID:C_ID + P]
        ones = CT[:, C_ONES:C_ONES + P]

        stats6 = sb("stats6", [P, TH, 6])
        mean, var, rstd = sb("mean", [P, TH]), sb("var", [P, TH]), sb("rstd", [P, TH])
        amean, arstd = sb("amean", [P, TILES]), sb("arstd", [P, TILES])
        msum, mdiff, msq, rough, rr = (sb(n, [P, TH]) for n in ("msum", "mdiff", "msq", "rough", "rr"))
        half_power = sb("half_power", [P, TH])

        xr = sb("xr", [P, 4, D])
        xrT = sb("xrT", [P, 4, P])
        logits = sb("logits", [P, TH, EXPERTS])
        te3 = [P, TH, EXPERTS]
        shifted, weight, score = sb("shifted", te3), sb("weight", te3), sb("score", te3)
        biased, found = sb("biased", te3), sb("found", te3)
        chosen = sb("chosen", [P, TOP_K, TH, EXPERTS])
        picked = sb("picked", [P, TOP_K, TH, EXPERTS])
        colmax, total = sb("colmax", [P, TH]), sb("total", [P, TH])
        coef = sb("coef", [P, TOP_K, TH])
        et3 = [P, EXPERTS, TH]
        taken, upto, place = sb("taken", et3), sb("upto", et3), sb("place", et3)
        rowsum = sb("rowsum", [P, EXPERTS])
        tiles_of, last_tile, start = (sb(n, [P, EXPERTS]) for n in ("tiles_of", "last_tile", "start"))
        over = sb("over", [P, EXPERTS, TH])
        passed = sb("passed", [P, NT, EXPERTS])
        slot_f = sb("slot_f", [P, TOP_K, TH])
        slot = [sb(f"slot{h}", [P, TOP_K, TH], I32) for h in range(HALVES)]
        expert_f = sb("expert_f", [P, NT])
        expert = [sb(f"expert{h}", [P, NT], I32) for h in range(HALVES)]
        rows = [sb(f"rows{h}", [P, TOP_K, TH, D]) for h in range(HALVES)]

        xe = sb("xe", [P, RING, D])
        xeT = sb("xeT", [P, 2, P])
        act1 = sb("act1", [P, 2, HIDDEN])
        hid = sb("hid", [P, 2, HP])
        hidT = sb("hidT", [P, 2, HP])
        ye = sb("ye", [P, RING, D])
        zeros = sb("zeros", [P, NT * 32])

        slots_in = [nc.dram_tensor(f"slots_in{h}", [NT * P, D], F32).ap() for h in range(HALVES)]
        slots_out = [nc.dram_tensor(f"slots_out{h}", [NT * P, D], F32).ap() for h in range(HALVES)]

        WQ, WK, WV, WO = (sb(n, [P, D]) for n in ("WQ", "WK", "WV", "WO"))
        identb = sb("identb", [P, P], BF16)
        xa, xaT = sb("xa", [P, 2, D]), sb("xaT", [P, SEQ])
        split = sb("split", [P, 2, 3, SEQ], BF16)
        resid = sb("resid", [P, 2, SEQ])
        QS = [sb(f"QS{q}", [P, PAIRS, 2, SEQ], BF16) for q in range(2)]
        KS = [sb(f"KS{q}", [P, PAIRS, SEQ], BF16) for q in range(2)]
        zrows = sb("zrows", [2, 4 * 2 * SEQ], BF16)
        V1 = [sb(f"V1_{q}", [P, 2, HEADS, 32]) for q in range(3)]
        PT = sb("PT", [P, 4, 2, SEQ])
        mx = sb("mx", [P, 2, PAIRS, 2])
        nm = sb("nm", [P, 2, 4 * PAIRS], BF16)
        nmT = sb("nmT", [4 * PAIRS, SEQ], BF16)
        oT = sb("oT", [P, HEADS // 4, SEQ])
        rsum, on = sb("rsum", [P, 2, HEADS]), sb("on", [P, 2, D])
        onT = sb("onT", [P, SEQ])
        scratch = nc.dram_tensor("stacks", [2, 2, 2, PAIRS, HD, NTERM, SEQ], BF16).ap()

        banks = ctx.enter_context(nc.psum_tensor("banks", [P, 8, 512], F32))
        PS = [banks[:, b, :] for b in range(8)]

        s_x = [sem(f"s_x{h}") for h in range(HALVES)]
        s_const = sem("s_const")
        s_w = sem("s_w")
        s_cleared = [sem(f"s_cleared{h}") for h in range(HALVES)]
        s_zero = sem("s_zero")
        s_dve = sem("s_dve")
        s_var, s_pow = sem("s_var"), sem("s_pow")
        s_xr, s_rt, s_rte, s_lg = sem("s_xr"), sem("s_rt"), sem("s_rte"), sem("s_lg")
        s_shift, s_exp = sem("s_shift"), sem("s_exp")
        s_rowsum, s_count = sem("s_rowsum"), sem("s_count")
        s_slot, s_rows, s_expert, s_lgread = sem("s_slot"), sem("s_rows"), sem("s_expert"), sem("s_lgread")
        s_scat = [sem(f"s_scat{h}") for h in range(HALVES)]
        s_xe = [sem(f"s_xe{r}") for r in range(RING)]
        s_xt, s_xte, s_u1, s_u3 = sem("s_xt"), sem("s_xte"), sem("s_u1"), sem("s_u3")
        s_act, s_hid, s_ht, s_hte = sem("s_act"), sem("s_hid"), sem("s_ht"), sem("s_hte")
        s_y, s_ye = sem("s_y"), sem("s_ye")
        s_st = [sem(f"s_st{r}") for r in range(RING)]
        GC = 4
        s_gath = [[sem(f"s_gath{h}_{c}") for c in range(GC)] for h in range(HALVES)]
        s_comb = sem("s_comb")
        s_out = sem("s_out")
        s_xa, s_at, s_ate, s_qk, s_v, s_ve = (sem(n) for n in ("s_xa", "s_at", "s_ate", "s_qk", "s_v", "s_ve"))
        s_hi, s_res, s_mid, s_lo, s_wr = (sem(n) for n in ("s_hi", "s_res", "s_mid", "s_lo", "s_wr"))
        s_stack = [[sem(f"s_stack{q}_{c}") for c in range(2)] for q in range(2)]
        s_mrow = [sem(f"s_mrow{q}") for q in range(2)]
        s_s, s_max, s_nm, s_nmt, s_nmte = (sem(n) for n in ("s_s", "s_max", "s_nm", "s_nmt", "s_nmte"))
        s_sc, s_exp2, s_av, s_ove = (sem(n) for n in ("s_sc", "s_exp2", "s_av", "s_ove"))
        s_ot, s_on, s_ont, s_onte, s_proj, s_add = (sem(n) for n in ("s_ot", "s_on", "s_ont", "s_onte",
                                                                     "s_proj", "s_add"))
        s_wa, s_vzero = sem("s_wa"), sem("s_vzero")

        chain = [0]

        def link(eng, ins):
            chain[0] += 1
            ins.then_inc(s_dve, 1)
            eng.wait_ge(s_dve, chain[0])

        block = ctx.enter_context(nc.Block())

        def norm_stats(eng, tiles, mean):
            for t in range(0, TH, 4):
                for i in range(t, t + 4):
                    chain[0] += 1
                    eng.bn_stats(stats6[:, i, :], tiles[:, i, :]).then_inc(s_dve, 1)
                yield
            eng.wait_ge(s_dve, chain[0])
            link(eng, eng.tensor_tensor(msum[:], stats6[:, :, 1], stats6[:, :, 4], ALU.add))
            link(eng, eng.tensor_tensor(mdiff[:], stats6[:, :, 1], stats6[:, :, 4], ALU.subtract))
            link(eng, eng.tensor_tensor(var[:], stats6[:, :, 2], stats6[:, :, 5], ALU.add))
            yield
            link(eng, eng.tensor_scalar(mean, msum[:], 0.5, None, ALU.mult))
            link(eng, eng.scalar_tensor_tensor(msq[:], mdiff[:], 0.25, mdiff[:], ALU.mult, ALU.mult))
            link(eng, eng.tensor_scalar(var[:], var[:], 1.0 / D, LN_EPS, ALU.mult, ALU.add))
            eng.tensor_tensor(var[:], var[:], msq[:], ALU.add).then_inc(s_var, 1)
            yield

        def norm_root(eng, n, rstd):
            yield
            eng.wait_ge(s_pow, n + 1)
            link(eng, eng.tensor_tensor(rr[:], rough[:], rough[:], ALU.mult))
            link(eng, eng.scalar_tensor_tensor(rr[:], rr[:], -0.5, var[:], ALU.mult, ALU.mult))
            link(eng, eng.scalar_tensor_tensor(rstd, rr[:], 1.5, rough[:], ALU.add, ALU.mult))
            yield

        def norm_of_attention(eng, h, n):
            tiles = slice(h * TH, (h + 1) * TH)
            yield from norm_stats(eng, X[:, tiles, :], amean[:, tiles])
            yield from norm_root(eng, n, arstd[:, tiles])

        def route_vector(eng, g, n, h):
            xh = X[:, h * TH:(h + 1) * TH, :]
            yield from norm_stats(eng, xh, mean[:])
            yield from norm_root(eng, n, rstd[:])
            for k in range(RG):
                if k:
                    eng.wait_ge(s_lg, RG * g + k)
                    eng.tensor_copy(logits[:, 4 * k - 4:4 * k, :],
                                    PS[7][:, 0:4 * EXPERTS].rearrange("p (t e) -> p t e", e=EXPERTS))\
                       .then_inc(s_lgread, 1)
                wait(eng, s_rt, RG * g + k)
                for i in range(4 * k, 4 * k + 4):
                    eng.tensor_scalar(xr[:, i % 4, :], xh[:, i, :], mean[:, i:i + 1], rstd[:, i:i + 1],
                                      ALU.subtract, ALU.mult).then_inc(s_xr, 1)
                for _ in range(4):
                    yield
            eng.wait_ge(s_lg, RG * (g + 1))
            eng.tensor_copy(logits[:, TH - 4:TH, :],
                            PS[7][:, 0:4 * EXPERTS].rearrange("p (t e) -> p t e", e=EXPERTS))\
               .then_inc(s_lgread, 1)
            eng.wait_ge(s_lgread, (RG + 1) * g + RG)
            over_e = lambda a: a.unsqueeze(2).to_broadcast([P, TH, EXPERTS])
            over_t = lambda a: a.unsqueeze(1).to_broadcast([P, TH, EXPERTS])
            rev = over_t(CT[:, C_REV:C_STEP])
            link(eng, eng.tensor_reduce(colmax[:], logits[:], AX.X, ALU.max))
            yield
            eng.tensor_tensor(shifted[:], logits[:], over_e(colmax[:, :]), ALU.subtract).then_inc(s_shift, 1)
            yield
            yield
            eng.wait_ge(s_exp, g + 1)
            link(eng, eng.tensor_reduce(total[:], weight[:], AX.X, ALU.add))
            link(eng, eng.reciprocal(total[:], total[:]))
            yield
            link(eng, eng.tensor_tensor(score[:], weight[:], over_e(total[:, :]), ALU.mult))
            link(eng, eng.tensor_tensor(biased[:], score[:], over_t(BIAS[:, :]), ALU.add))
            yield
            for k in range(TOP_K):
                link(eng, eng.tensor_reduce(colmax[:], biased[:], AX.X, ALU.max))
                link(eng, eng.tensor_tensor(found[:], biased[:], over_e(colmax[:, :]), ALU.is_equal))
                yield
                link(eng, eng.tensor_tensor(found[:], found[:], rev, ALU.mult))
                link(eng, eng.tensor_reduce(colmax[:], found[:], AX.X, ALU.max))
                yield
                link(eng, eng.tensor_tensor(chosen[:, k], rev, over_e(colmax[:, :]), ALU.is_equal))
                if k + 1 < TOP_K:
                    link(eng, eng.scalar_tensor_tensor(biased[:], chosen[:, k], -FAR, biased[:],
                                                       ALU.mult, ALU.add))
                yield
            link(eng, eng.tensor_tensor(taken[:].rearrange("p e t -> p t e"), chosen[:, 0], chosen[:, 1],
                                        ALU.add))
            eng.tensor_reduce(rowsum[:], taken[:], AX.X, ALU.add).then_inc(s_rowsum, 1)
            yield
            for k in range(TOP_K):
                link(eng, eng.tensor_tensor(picked[:, k], chosen[:, k], score[:], ALU.mult))
            yield
            link(eng, eng.tensor_reduce(coef[:], picked[:], AX.X, ALU.add))
            for k in range(TOP_K):
                link(eng, eng.tensor_tensor(coef[:, k], coef[:, k], rstd[:], ALU.mult))
            yield
            flat = lambda a: a[:].rearrange("p e t -> p (e t)")
            link(eng, eng.tensor_tensor_scan(flat(upto), CT[:, C_SEG:C_END], flat(taken), 0.0,
                                             ALU.mult, ALU.add))
            link(eng, eng.tensor_tensor(place[:], upto[:], taken[:], ALU.subtract))
            yield
            eng.wait_ge(s_count, g + 1)
            before, counts = PS[7][:, 0:EXPERTS], PS[7][:, EXPERTS:2 * EXPERTS]
            et = [P, EXPERTS, TH]
            link(eng, eng.tensor_tensor(over[:], counts.unsqueeze(2).to_broadcast(et),
                                        CT[:, C_STEP:C_TILE].unsqueeze(1).to_broadcast(et), ALU.is_gt))
            link(eng, eng.tensor_reduce(tiles_of[:], over[:], AX.X, ALU.add))
            yield
            link(eng, eng.tensor_tensor_scan(last_tile[:], CT[:, C_ONES:C_ONES + EXPERTS], tiles_of[:],
                                             0.0, ALU.mult, ALU.add))
            link(eng, eng.tensor_tensor(start[:], last_tile[:], tiles_of[:], ALU.subtract))
            eng.scalar_tensor_tensor(start[:], start[:], float(P), before, ALU.mult, ALU.add).then_inc(s_lgread, 1)
            eng.wait_ge(s_lgread, (RG + 1) * (g + 1))
            yield
            link(eng, eng.tensor_tensor(place[:], place[:], start[:, :].unsqueeze(2).to_broadcast(et), ALU.add))
            for k in range(TOP_K):
                link(eng, eng.tensor_tensor(picked[:, k], chosen[:, k],
                                            place[:].rearrange("p e t -> p t e"), ALU.mult))
            yield
            link(eng, eng.tensor_reduce(slot_f[:], picked[:], AX.X, ALU.add))
            eng.tensor_copy(slot[h][:], slot_f[:]).then_inc(s_slot, 1)
            yield
            for k in range(TOP_K):
                for i in range(TH):
                    eng.tensor_scalar(rows[h][:, k, i, :], xh[:, i, :], mean[:, i:i + 1],
                                      coef[:, k, i:i + 1], ALU.subtract, ALU.mult).then_inc(s_rows, 1)
                    if i % 4 == 3:
                        yield
            ne = [P, NT, EXPERTS]
            link(eng, eng.tensor_tensor(passed[:], CT[:, C_TILE:C_SEG].unsqueeze(2).to_broadcast(ne),
                                        last_tile[:, :].unsqueeze(1).to_broadcast(ne), ALU.is_ge))
            yield
            link(eng, eng.tensor_reduce(expert_f[:], passed[:], AX.X, ALU.add))
            link(eng, eng.tensor_scalar(expert_f[:], expert_f[:], float(EXPERTS - 1), None, ALU.min))
            eng.tensor_copy(expert[h][:], expert_f[:]).then_inc(s_expert, 1)
            yield

        def route_tensor(eng, g):
            for _ in range(9):
                yield
            for k in range(RG):
                eng.wait_ge(s_xr, TH * g + 4 * k + 4)
                wait(eng, s_lgread, (RG + 1) * g + k)
                for i in range(4):
                    last = eng.transpose(PS[7][:, i * P:(i + 1) * P], xr[:, i, :], ident)
                last.then_inc(s_rt, 1)
                yield
                yield
                eng.wait_ge(s_rte, RG * g + k + 1)
                for i in range(4):
                    last = eng.matmul(PS[7][:, i * EXPERTS:(i + 1) * EXPERTS], xrT[:, i, :], GATE[:],
                                      start=True, stop=True)
                last.then_inc(s_lg, 1)
                yield
                yield
            for _ in range(12):
                yield
            eng.wait_ge(s_rowsum, g + 1)
            eng.matmul(PS[7][:, 0:EXPERTS], CT[:, C_BEFORE:C_BEFORE + P], rowsum[:], start=True, stop=True)
            eng.matmul(PS[7][:, EXPERTS:2 * EXPERTS], ones, rowsum[:], start=True, stop=True)\
               .then_inc(s_count, 1)
            yield

        def route_scalar(eng, g):
            for _ in range(10):
                yield
            for k in range(RG):
                eng.wait_ge(s_rt, RG * g + k + 1)
                wait(eng, s_lg, RG * g + k)
                eng.copy(xrT[:].rearrange("p t n -> p (t n)"), PS[7]).then_inc(s_rte, 1)
                for _ in range(4):
                    yield
            eng.wait_ge(s_shift, g + 1)
            eng.activation(weight[:], shifted[:], ACT.Exp).then_inc(s_exp, 1)
            yield

        def root_gpsimd(eng, n):
            eng.wait_ge(s_var, n + 1)
            eng.tensor_tensor(rough[:], var[:], half_power[:], ALU.pow).then_inc(s_pow, 1)

        def scatter_gpsimd(eng, g, h):
            if g < HALVES:
                eng.wait_ge(s_cleared[h], 16)
            eng.wait_ge(s_slot, g + 1)
            for k in range(TOP_K):
                for t in range(TH):
                    if t % 4 == 0:
                        eng.wait_ge(s_rows, (TOP_K * g + k) * TH + t + 4)
                    eng.indirect_dma_start(slots_in[h], bass.IndirectOffsetOnAxis(ap=slot[h][:, k, t:t + 1], axis=0),
                                           rows[h][:, k, t, :], None).then_inc(s_scat[h], 16)

        def gather_gpsimd(eng, g, h):
            for r in range(RING):
                eng.wait_ge(s_st[r], 16 * stored(g + 1, r))
            per = TH // GC
            for c in range(GC):
                for t in range(c * per, (c + 1) * per):
                    for k in range(TOP_K):
                        eng.indirect_dma_start(rows[h][:, k, t, :], None, slots_out[h],
                                               bass.IndirectOffsetOnAxis(ap=slot[h][:, k, t:t + 1], axis=0))\
                           .then_inc(s_gath[h][c], 16)

        def combine_vector(eng, g, h):
            per = TH // GC
            for c in range(GC):
                eng.wait_ge(s_gath[h][c], 16 * TOP_K * per * (g // HALVES + 1))
                a, b = (rows[h][:, k, c * per:(c + 1) * per, :] for k in range(TOP_K))
                xc = X[:, h * TH + c * per:h * TH + (c + 1) * per, :]
                link(eng, eng.tensor_tensor(a, a, b, ALU.add))
                yield
                eng.scalar_tensor_tensor(xc, a, 0.5, xc, ALU.mult, ALU.add).then_inc(s_comb, 1)
                yield
            eng.wait_ge(s_comb, GC * (g + 1))

        def stored(g, r):
            return g * len(range(r, NT, RING))

        def expert_sync(eng, g, h):
            b = g * NT
            eng.wait_ge(s_scat[h], 16 * TOP_K * TH * (g // HALVES + 1))
            lag = RING + 2

            def body(i, r, j):
                fixed = isinstance(i, int)
                if not fixed or i < NT:
                    wait(eng, s_xt, b + i - RING + 1)
                    eng.dma_start(xe[:, r, :], slots_in[h][bass.ds(i * P, P), :]).then_inc(s_xe[r], 16)
                if not fixed or i >= lag:
                    eng.wait_ge(s_ye, b + i - lag + 1)
                    q = (r - lag) % RING
                    eng.dma_start(slots_out[h][bass.ds((i - lag) * P, P), :], ye[:, q, :]).then_inc(s_st[q], 16)

            steps(eng, 0, NT + lag, 2 * RING, NT, body, RING)

        def expert_tensor(eng, g, h, side, ticks):
            b = g * NT

            def number(i):
                return eng.value_load(expert[h][0:1, bass.ds(i, 1)], min_val=0, max_val=EXPERTS - 1)

            def turn(i, r, j):
                eng.wait_ge(s_xe[r], 16 * (stored(g, r) + 1 + j))
                wait(eng, s_xte, b + i)
                eng.transpose(PS[0][:, 0:P], xe[:, r, :], ident).then_inc(s_xt, 1)

            def up(i, r):
                e = number(i)
                eng.wait_ge(s_xte, b + i + 1)
                wait(eng, s_act, b + i - 1)
                eng.matmul(PS[2 + r][:, 0:HIDDEN], xeT[:, r, :], one(W1[:, :, :], e), start=True, stop=True)\
                   .then_inc(s_u1, 1)
                wait(eng, s_hid, b + i - 1)
                eng.matmul(PS[4 + r][:, 0:HIDDEN], xeT[:, r, :], one(W3[:, :, :], e), start=True, stop=True)\
                   .then_inc(s_u3, 1)

            def down(i, r):
                e = number(i)
                eng.wait_ge(s_hte, b + i + 1)
                wait(eng, s_ye, b + i)
                for c in range(HC):
                    last = eng.matmul(PS[1][:, 0:D], hidT[:, r, c * P:(c + 1) * P], one(W2[:, :, c, :], e),
                                      start=c == 0, stop=c == HC - 1)
                last.then_inc(s_y, 1)

            def turn_hidden(i, r):
                eng.wait_ge(s_hid, b + i + 1)
                wait(eng, s_hte, b + i)
                for c in range(HC):
                    last = eng.transpose(PS[6][:, c * P:(c + 1) * P], hid[:, r, c * P:(c + 1) * P], ident)
                last.then_inc(s_ht, 1)

            def body(i, r, j):
                fixed = isinstance(i, int)
                if not fixed or -1 <= i < NT - 1:
                    turn(i + 1, (r + 1) % RING, j + (r + 1) // RING)
                if not fixed or 0 <= i < NT:
                    up(i, r % 2)
                if not fixed or 2 <= i:
                    down(i - 2, r % 2)
                if not fixed or 1 <= i <= NT:
                    turn_hidden(i - 1, 1 - r % 2)
                advance(side, ticks, i)

            if g == 0:
                eng.wait_ge(s_w, 16 * (3 + EXPERTS))
            eng.wait_ge(s_expert, g + 1)
            steps(eng, -1, NT + 2, RING, NT - 1, body, RING)

        def expert_scalar(eng, g, side, ticks):
            b = g * NT

            def body(i, r, j):
                fixed = isinstance(i, int)
                if not fixed or -1 <= i < NT - 1:
                    eng.wait_ge(s_xt, b + i + 2)
                    wait(eng, s_u3, b + i)
                    eng.copy(xeT[:, 1 - r % 2, :], PS[0][:, 0:P]).then_inc(s_xte, 1)
                if not fixed or 0 <= i < NT:
                    eng.wait_ge(s_u1, b + i + 1)
                    wait(eng, s_hid, b + i - 1)
                    eng.activation(act1[:, r % 2, :], PS[2 + r % 2][:, 0:HIDDEN], ACT.Silu).then_inc(s_act, 1)
                if not fixed or 2 <= i:
                    q, before = (r - 2) % RING, j + (r - 2) // RING
                    eng.wait_ge(s_y, b + i - 1)
                    wait(eng, s_st[q], 16 * (stored(g, q) + before))
                    eng.copy(ye[:, q, :], PS[1][:, 0:D]).then_inc(s_ye, 1)
                advance(side, ticks, i)

            steps(eng, -1, NT + 2, RING, NT - 1, body, RING)

        def expert_vector(eng, g, side, ticks):
            b = g * NT

            def body(i, r, j):
                fixed = isinstance(i, int)
                if not fixed or i < NT:
                    eng.wait_ge(s_act, b + i + 1)
                    eng.wait_ge(s_u3, b + i + 1)
                    wait(eng, s_ht, b + i - 1)
                    eng.tensor_tensor(hid[:, r % 2, 0:HIDDEN], PS[4 + r % 2][:, 0:HIDDEN], act1[:, r % 2, :], ALU.mult)\
                       .then_inc(s_hid, 1)
                if not fixed or i >= 1:
                    eng.wait_ge(s_ht, b + i)
                    wait(eng, s_y, b + i - 2)
                    eng.tensor_copy(hidT[:, 1 - r % 2, :], PS[6][:, 0:HP]).then_inc(s_hte, 1)
                advance(side, ticks, i)

            steps(eng, 0, NT + 1, RING, NT - 1, body, RING)

        FILLS = ((2, 5), (5, 8), (8, 10), (10, 13), (13, 16), (), (), (0, 2))
        scale = float(HD) ** -0.5

        def fills(n, u):
            m = n + 1 + u // (PAIRS - 1)
            return [(m, f, f // 2, f % 2) for f in range(*FILLS[u])] if FILLS[u] and 0 <= m < BATCH else []

        def attention_tensor(eng, side, ticks):
            for n in range(-2, BATCH + 1):
                ahead, nxt, now, done = (0 <= n + 2 < BATCH, 0 <= n + 1 < BATCH, 0 <= n < BATCH, 0 <= n - 1 < BATCH)
                for u in range(PAIRS):
                    fill = maxima_scores(eng, fills(n, u))
                    next(fill, None)
                    if now:
                        q = n % 2
                        if u == 0:
                            eng.wait_ge(s_mrow[q], 32 * (n // 2 + 1))
                        for kt in range(2):
                            f = 2 * (PAIRS * n + u) + kt
                            wait(eng, s_exp2, f - 2)
                            eng.matmul(PS[f % 3], KS[q][:, u, kt * P:(kt + 1) * P],
                                       QS[q][:, u, :, :].rearrange("p e n -> p (e n)"),
                                       start=True, stop=True).then_inc(s_sc, 1)
                    next(fill, None)
                    if now and u > 0:
                        values(eng, n, u - 1)
                    next(fill, None)
                    if ahead and u == 0:
                        m = n + 2
                        eng.wait_ge(s_xa, 2 * (m + 1))
                        wait(eng, s_ve, m)
                        wait(eng, s_nmte, n + 1)
                        wait(eng, s_add, n - 1)
                        for i in range(2):
                            last = eng.transpose(PS[6][:, i * P:(i + 1) * P], xa[:, i, :], ident)
                        last.then_inc(s_at, 1)
                    if ahead and u == 1:
                        eng.wait_ge(s_ate, n + 3)
                        for part, w in enumerate((WQ, WK)):
                            last = eng.matmul(PS[6][:, part * SEQ:(part + 1) * SEQ], w[:], xaT[:],
                                              start=True, stop=True)
                        last.then_inc(s_qk, 1)
                    if ahead and u == 2:
                        eng.wait_ge(s_res, n + 3)
                        for kt in range(2):
                            last = eng.matmul(PS[6][:, kt * P:(kt + 1) * P], xaT[:, kt * P:(kt + 1) * P], WV[:],
                                              start=True, stop=True)
                        last.then_inc(s_v, 1)
                    if done and u in (3, 4):
                        qt = u - 3
                        eng.wait_ge(s_ove, 2 * n)
                        if u == 3:
                            eng.wait_ge(s_ve, min(n + 3, BATCH))
                            eng.wait_ge(s_nmte, min(n + 1, BATCH))
                            wait(eng, s_add, n - 1)
                        else:
                            eng.wait_ge(s_on, 2 * n - 1)
                        for c in range(HEADS // 4):
                            last = eng.transpose(PS[6][:, c * P:(c + 1) * P], oT[:, c, qt * P:(qt + 1) * P], ident)
                        last.then_inc(s_ot, 1)
                    if done and u == 6:
                        eng.wait_ge(s_on, 2 * n)
                        if nxt:
                            eng.wait_ge(s_nmte, n + 2)
                        for qt in range(2):
                            last = eng.transpose(PS[6][:, qt * P:(qt + 1) * P], on[:, qt, :], ident)
                        last.then_inc(s_ont, 1)
                    if nxt and u == 5:
                        eng.wait_ge(s_nm, n + 2)
                        if done:
                            eng.wait_ge(s_on, 2 * n)
                        elif ahead:
                            eng.wait_ge(s_ve, n + 3)
                        for qt in range(2):
                            last = eng.transpose(PS[6][0:4 * PAIRS, :].bitcast(BF16)[:, qt * P:(qt + 1) * P],
                                                 nm[:, qt, :], identb[:])
                        last.then_inc(s_nmt, 1)
                    if done and u == 7:
                        eng.wait_ge(s_onte, n)
                        for qt in range(2):
                            last = eng.matmul(PS[6][:, qt * P:(qt + 1) * P], onT[:, qt * P:(qt + 1) * P], WO[:],
                                              start=True, stop=True)
                        last.then_inc(s_proj, 1)
                    if now and u == PAIRS - 1:
                        values(eng, n, u)
                    advance(side, ticks, PAIRS * n + u)

        def maxima_scores(eng, todo):
            for m, f, pair, qt in todo:
                q = m % 2
                if f % 8 == 0:
                    eng.wait_ge(s_stack[q][f // 8], 80 * (m // 2 + 1))
                wait(eng, s_max, 2 * PAIRS * m + f - 1)
                for e in range(2):
                    last = eng.matmul(PS[3 + f % 2][:, e * SEQ:(e + 1) * SEQ],
                                      QS[q][:, pair, e, qt * P:(qt + 1) * P], KS[q][:, pair, :],
                                      start=True, stop=True)
                last.then_inc(s_s, 1)
                yield

        def values(eng, n, u):
            eng.wait_ge(s_exp2, 2 * (PAIRS * n + u + 1))
            if u == 0:
                eng.wait_ge(s_ve, n + 1)
            if u % 4 == 0:
                wait(eng, s_ove, 2 * n + u // 4)
            for e in range(2):
                j = (2 * u + e) % 4
                for kt in range(2):
                    last = eng.matmul(PS[5][32 * j:32 * j + 32, (u // 2 % 2) * SEQ:(u // 2 % 2 + 1) * SEQ],
                                      V1[n % 3][:, kt, 2 * u + e, :], PT[:, 2 * (u % 2) + kt, e, :],
                                      start=kt == 0, stop=kt == 1, tile_position=(0, 32 * j))
            last.then_inc(s_av, 1)

        def attention_scalar(eng, side, ticks):
            for n in range(-2, BATCH + 1):
                ahead, nxt, now, done = (0 <= n + 2 < BATCH, 0 <= n + 1 < BATCH, 0 <= n < BATCH, 0 <= n - 1 < BATCH)
                for u in range(PAIRS):
                    if now:
                        wait(eng, s_av, PAIRS * n + u - 1)
                        for kt in range(2):
                            f = 2 * (PAIRS * n + u) + kt
                            eng.wait_ge(s_sc, f + 1)
                            eng.activation(PT[:, f % 4].rearrange("p e n -> p (e n)"), PS[f % 3], ACT.Exp,
                                           scale=scale).then_inc(s_exp2, 1)
                    if u == 0 and done:
                        read_values(eng, n - 1, 1)
                    if u == 4 and now:
                        read_values(eng, n, 0)
                    if u == 0 and ahead:
                        eng.wait_ge(s_at, n + 3)
                        wait(eng, s_v, n + 2)
                        eng.copy(xaT[:], PS[6][:, 0:SEQ]).then_inc(s_ate, 1)
                    if u == 1 and ahead:
                        eng.wait_ge(s_qk, n + 3)
                        wait(eng, s_wr, 64 * (n + 2))
                        eng.copy(split[:, :, 0, :], PS[6][:, :].rearrange("p (s n) -> p s n", s=2)).then_inc(s_hi, 1)
                    if u == 2 and ahead:
                        eng.wait_ge(s_res, n + 3)
                        eng.copy(split[:, :, 1, :], resid[:, :, :]).then_inc(s_mid, 1)
                        q = (n + 2) % 3
                        eng.wait_ge(s_v, n + 3)
                        wait(eng, s_av, PAIRS * n)
                        eng.copy(V1[q][:, :, :, 0:HD],
                                 PS[6][:, 0:2 * P].rearrange("p (k a d) -> p k a d", k=2, d=HD)).then_inc(s_ve, 1)
                    if u == 6 and done:
                        eng.wait_ge(s_ont, n)
                        wait(eng, s_proj, n - 1)
                        eng.copy(onT[:], PS[6][:, 0:SEQ]).then_inc(s_onte, 1)
                    if u == 5 and nxt:
                        eng.wait_ge(s_nmt, n + 2)
                        if n + 1 > 0:
                            p = n % 2
                            eng.wait_ge(s_mrow[p], 32 * (n // 2 + 1))
                        eng.copy(nmT[:], PS[6][0:4 * PAIRS, :].bitcast(BF16)[:, 0:SEQ]).then_inc(s_nmte, 1)
                    advance(side, ticks, PAIRS * n + u)

        def read_values(eng, n, i):
            eng.wait_ge(s_av, PAIRS * n + 4 * (i + 1))
            wait(eng, s_ot, 2 * n)
            eng.copy(oT[:, 2 * i:2 * i + 2, :].rearrange("p c n -> p (c n)"), PS[5][:, :]).then_inc(s_ove, 1)

        def normed_pair(eng, n):
            wait(eng, s_at, n)
            for i in range(2):
                t = 2 * n + i
                eng.tensor_scalar(xa[:, i, :], X[:, t, :], amean[:, t:t + 1], arstd[:, t:t + 1],
                                  ALU.subtract, ALU.mult).then_inc(s_xa, 1)

        def attention_vector(eng, side, ticks):
            normed_pair(eng, 0)
            for n in range(-2, BATCH + 1):
                ahead, nxt, now, done = (0 <= n + 2 < BATCH, 0 <= n + 1 < BATCH, 0 <= n < BATCH, 0 <= n - 1 < BATCH)
                for u in range(PAIRS):
                    if u == 2 and ahead:
                        eng.wait_ge(s_hi, n + 3)
                        eng.tensor_tensor(resid[:], PS[6][:, :].rearrange("p (s n) -> p s n", s=2),
                                          split[:, :, 0, :], ALU.subtract).then_inc(s_res, 1)
                    for m, f, pair, qt in fills(n, u):
                        eng.wait_ge(s_s, 2 * PAIRS * m + f + 1)
                        if f == 0:
                            wait(eng, s_nm, m)
                        eng.tensor_reduce(mx[:, qt, pair, :], PS[3 + f % 2][:, :].rearrange("p (e n) -> p e n", e=2),
                                          AX.X, ALU.max).then_inc(s_max, 1)
                    if u == 2 and ahead:
                        eng.wait_ge(s_mid, n + 3)
                        eng.tensor_tensor(split[:, :, 2, :], resid[:], split[:, :, 1, :], ALU.subtract).then_inc(s_lo, 1)
                    if u in (3, 4) and done:
                        qt = u - 3
                        eng.wait_ge(s_ot, 2 * n - 1 + qt)
                        sums = PS[6][:, :].rearrange("p (a c) -> p a c", c=32)
                        link(eng, eng.reciprocal(rsum[:, qt, :], sums[:, :, HD]))
                        wait(eng, s_ont, n - 1)
                        eng.tensor_tensor(on[:, qt, :].rearrange("p (a d) -> p a d", d=HD), sums[:, :, 0:HD],
                                          rsum[:, qt, :].unsqueeze(2).to_broadcast([P, HEADS, HD]),
                                          ALU.mult).then_inc(s_on, 1)
                    if u == 4 and nxt:
                        eng.wait_ge(s_max, 2 * PAIRS * (n + 2))
                        wait(eng, s_nmt, n + 1)
                        m4 = mx[:].rearrange("p q r e -> p q (r e)")
                        n4 = nm[:].rearrange("p q (t m) -> p q t m", t=2)
                        link(eng, eng.tensor_scalar(n4[:, :, 0, :], m4, -1.0, None, ALU.mult))
                        eng.scalar_tensor_tensor(n4[:, :, 1, :], m4, -1.0, n4[:, :, 0, :], ALU.mult,
                                                 ALU.subtract).then_inc(s_nm, 1)
                    if u == 6 and 0 <= n + 3 < BATCH:
                        normed_pair(eng, n + 3)
                    if u == 7 and done:
                        eng.wait_ge(s_proj, n)
                        xb = X[:, 2 * n - 2:2 * n, :]
                        eng.tensor_tensor(xb, PS[6][:, 0:SEQ].rearrange("p (q n) -> p q n", q=2), xb,
                                          ALU.add).then_inc(s_add, 1)
                    advance(side, ticks, PAIRS * n + u)

        def attention_sync(eng):
            for n in range(-2, BATCH):
                if n + 2 < BATCH:
                    m, q = n + 2, n % 2
                    eng.wait_ge(s_lo, m + 1)
                    if m >= 2:
                        for c in range(2):
                            eng.wait_ge(s_stack[q][c], 80 * (m // 2))
                    flat = scratch[q].rearrange("s e r d t n -> s (e r d) t n")
                    for s, reps in ((0, 2), (1, 3)):
                        parts = 6 // reps
                        eng.dma_start(flat[s, :, 0:6, :].rearrange("c (a b) n -> c a (b n)", a=reps),
                                      split[:, s, 0:parts, :].rearrange("c b n -> c (b n)").unsqueeze(1)
                                      .to_broadcast([P, reps, parts * SEQ])).then_inc(s_wr, 16)
                    eng.dma_start(flat[0, :, 6, :], split[:, 0, 0, :]).then_inc(s_wr, 16)
                    eng.dma_start(flat[1, :, 6, :], split[:, 1, 2, :]).then_inc(s_wr, 16)
                    eng.wait_ge(s_wr, 64 * (m + 1))
                    stack(eng, n, m, 0)
                if 0 <= n + 1 < BATCH:
                    m, q = n + 1, (n + 1) % 2
                    eng.wait_ge(s_nmte, m + 1)
                    for t in range(2):
                        eng.dma_start(QS[q][STACK + t:STACK + t + 1].rearrange("p r e n -> p (r e) n"),
                                      nmT[2 * PAIRS * t:2 * PAIRS * (t + 1), :]).then_inc(s_mrow[q], 16)
                if n + 2 < BATCH:
                    stack(eng, n, n + 2, 1)

        def stack(eng, n, m, c):
            q = m % 2
            wait(eng, s_sc, 2 * (PAIRS * n + 4 * (c + 1)))
            pairs = slice(4 * c, 4 * c + 4)
            for e in range(2):
                for side, dst in ((0, QS[q][:, pairs, e, :]), (1, KS[q][:, pairs, :])):
                    eng.dma_start(dst[e * STACK // 2:(e + 1) * STACK // 2],
                                  scratch[q, side, e, pairs].rearrange("r d t n -> (d t) r n"))\
                       .then_inc(s_stack[q][c], 16)
            eng.dma_start(QS[q][STACK:STACK + 2, pairs, :, :].rearrange("p r e n -> p (r e n)"), zrows[:])\
               .then_inc(s_stack[q][c], 16)


        @block.sync
        def _(sp):
            xv = x.rearrange("(t p) d -> p t d", p=P)
            sp.dma_start(CT[:], consts).then_inc(s_const, 16)
            sp.dma_start(X[:, 0:TH, :], xv[:, 0:TH, :]).then_inc(s_x[0], 16)
            sp.dma_start(GATE[:], gate).then_inc(s_const, 16)
            sp.dma_start(BIAS[:], bias.partition_broadcast(P)).then_inc(s_const, 16)
            sp.dma_start(X[:, TH:TILES, :], xv[:, TH:TILES, :]).then_inc(s_x[1], 16)
            sp.wait_ge(s_zero, 1)
            for h in range(HALVES):
                sp.dma_start(slots_in[h].rearrange("(p r) d -> p (r d)", p=P).rearrange("p (a n) -> p a n", a=4),
                             zeros[:, :].unsqueeze(1).to_broadcast([P, 4, NT * 32])).then_inc(s_cleared[h], 16)
            sp.dma_start(W1[:], w1.rearrange("e d h -> d e h")).then_inc(s_w, 16)
            sp.dma_start(W3[:], w3.rearrange("e d h -> d e h")).then_inc(s_w, 16)
            full = HIDDEN // P * P
            for e in range(EXPERTS):
                sp.dma_start(W2[:, e, 0:HC - 1, :], w2[e, 0:full, :].rearrange("(c p) d -> p c d", p=P))\
                  .then_inc(s_w, 16)
            sp.wait_ge(s_zero, 4)
            sp.dma_start(W2[0:HIDDEN - full, :, HC - 1, :], w2[:, full:HIDDEN, :].rearrange("e p d -> p e d"))\
              .then_inc(s_w, 16)
            for w, a in ((WQ, wq), (WK, wk), (WV, wv), (WO, wo)):
                sp.dma_start(w[:], a).then_inc(s_wa, 16)
            ov = out.rearrange("(t p) d -> p t d", p=P)
            expert_sync(sp, 0, 0)
            expert_sync(sp, 1, 1)
            attention_sync(sp)
            expert_sync(sp, 2, 0)
            expert_sync(sp, 3, 1)
            for h in range(HALVES):
                for c in range(GC):
                    tiles = slice(h * TH + c * TH // GC, h * TH + (c + 1) * TH // GC)
                    sp.wait_ge(s_comb, GC * (HALVES + h) + c + 1)
                    sp.dma_start(ov[:, tiles, :], X[:, tiles, :]).then_inc(s_out, 16)
            sp.wait_ge(s_out, 16 * HALVES * GC)

        @block.gpsimd
        def _(pool):
            pool.memset(zeros[:], 0.0).then_inc(s_zero, 1)
            pool.memset(half_power[:], -0.5).then_inc(s_zero, 1)
            pool.memset(hid[:, :, HIDDEN:HP], 0.0).then_inc(s_zero, 1)
            pool.wait_ge(s_zero, 3)
            pool.memset(W2[HIDDEN % P:P, :, HC - 1, :], 0.0).then_inc(s_zero, 1)
            pool.wait_ge(s_zero, 4)
            root_gpsimd(pool, 0)
            scatter_gpsimd(pool, 0, 0)
            root_gpsimd(pool, 1)
            scatter_gpsimd(pool, 1, 1)
            gather_gpsimd(pool, 0, 0)
            root_gpsimd(pool, 2)
            gather_gpsimd(pool, 1, 1)
            root_gpsimd(pool, 3)
            root_gpsimd(pool, 4)
            scatter_gpsimd(pool, 2, 0)
            root_gpsimd(pool, 5)
            scatter_gpsimd(pool, 3, 1)
            gather_gpsimd(pool, 2, 0)
            gather_gpsimd(pool, 3, 1)

        def none(i):
            return 0

        def late(i):
            return int(i >= 22)

        def twice(i):
            return 2 if i >= 0 else 0

        def in_attention(i):
            if i < PAIRS * (NB + 1):
                return int(i >= 3 * PAIRS)
            return 2 if i >= 0 else 0

        def idle(ticks):
            for _ in range(ticks):
                yield

        @block.scalar
        def _(act):
            for g in range(HALVES):
                for _ in route_scalar(act, g):
                    pass
            expert_scalar(act, 0, idle(0), none)
            expert_scalar(act, 1, idle(0), none)
            side = chained(idle(SIDE), route_scalar(act, 2))
            attention_scalar(act, side, in_attention)
            for _ in side:
                pass
            side = route_scalar(act, 3)
            expert_scalar(act, 2, side, twice)
            expert_scalar(act, 3, side, none)

        @block.tensor
        def _(pe):
            pe.wait_ge(s_const, 48)
            for g in range(HALVES):
                for _ in route_tensor(pe, g):
                    pass
            pe.wait_ge(s_zero, 4)
            expert_tensor(pe, 0, 0, idle(0), none)
            expert_tensor(pe, 1, 1, idle(0), none)
            pe.wait_ge(s_wa, 64)
            pe.wait_ge(s_vzero, 8)
            pe.wait_ge(s_ye, 2 * NT)
            pe.wait_ge(s_hte, 2 * NT)
            side = chained(idle(SIDE), route_tensor(pe, 2))
            attention_tensor(pe, side, in_attention)
            for _ in side:
                pass
            pe.wait_ge(s_exp2, 2 * PAIRS * BATCH)
            pe.wait_ge(s_ove, 2 * BATCH)
            pe.wait_ge(s_add, BATCH)
            side = route_tensor(pe, 3)
            expert_tensor(pe, 2, 0, side, twice)
            expert_tensor(pe, 3, 1, side, none)

        @block.vector
        def _(dve):
            dve.wait_ge(s_const, 48)
            for h in range(HALVES):
                dve.wait_ge(s_x[h], 16)
                for _ in route_vector(dve, h, h, h):
                    pass
            for q in range(2):
                dve.memset(QS[q][:].rearrange("p r e n -> p (r e n)").bitcast(F32), 0.0).then_inc(s_vzero, 1)
                dve.memset(KS[q][STACK // 32 * 32:P], 1.0).then_inc(s_vzero, 1)
            for q in range(3):
                dve.memset(V1[q][:, :, :, HD:32], 0.0).then_inc(s_vzero, 1)
            dve.memset(zrows[:], 0.0).then_inc(s_vzero, 1)
            dve.wait_ge(s_vzero, 8)
            for q in range(3):
                link(dve, dve.memset(V1[q][:, :, :, HD:HD + 1], 1.0))
            link(dve, dve.tensor_copy(identb[:], ident))
            expert_vector(dve, 0, idle(0), none)
            side = chained(combine_vector(dve, 0, 0), norm_of_attention(dve, 0, 2))
            expert_vector(dve, 1, side, late)
            for _ in side:
                pass
            side = chained(combine_vector(dve, 1, 1), norm_of_attention(dve, 1, 3),
                           idle(SIDE - 2 * GC - TH // 4 - 4), route_vector(dve, 2, 4, 0))
            attention_vector(dve, side, in_attention)
            for _ in side:
                pass
            dve.wait_ge(s_add, BATCH)
            side = route_vector(dve, 3, 5, 1)
            expert_vector(dve, 2, side, twice)
            for _ in side:
                pass
            expert_vector(dve, 3, idle(0), none)
            for h in range(HALVES):
                for _ in combine_vector(dve, 2 + h, h):
                    pass


def chained(*programs):
    for p in programs:
        yield from p


def kernel(L0_attn_hidden_states, L0_attn_Wq, L0_attn_Wk, L0_attn_Wv, L0_attn_Wo, L0_ffn_gate_w,
           L0_ffn_expert_bias, L0_ffn_w1, L0_ffn_w2, L0_ffn_w3):
    import concourse.bacc as bacc
    from concourse.bass_utils import run_bass_kernel_spmd

    def turned(w):
        return np.ascontiguousarray(np.asarray(w).T)

    def by_parity(w):
        w = np.asarray(w).reshape(PAIRS, 2, HD, D)
        return np.ascontiguousarray(w.transpose(3, 1, 0, 2).reshape(D, D))

    arrays = {
        "x": np.ascontiguousarray(L0_attn_hidden_states).reshape(BATCH * SEQ, D),
        "wq": by_parity(L0_attn_Wq), "wk": by_parity(L0_attn_Wk),
        "wv": turned(L0_attn_Wv), "wo": turned(L0_attn_Wo),
        "gate": turned(L0_ffn_gate_w), "bias": np.ascontiguousarray(L0_ffn_expert_bias),
        "w1": np.ascontiguousarray(L0_ffn_w1), "w2": np.ascontiguousarray(L0_ffn_w2),
        "w3": np.ascontiguousarray(L0_ffn_w3), "consts": constants(),
    }
    nc = bacc.Bacc("TRN2", target_bir_lowering=False, num_devices=1)
    aps = {n: nc.dram_tensor(f"in_{n}", a.shape, mybir.dt.from_np(a.dtype), kind="ExternalInput").ap()
           for n, a in arrays.items()}
    out = nc.dram_tensor("out_0", [BATCH * SEQ, D], F32, kind="ExternalOutput").ap()
    build(nc, *aps.values(), out)
    r = run_bass_kernel_spmd(nc, [{f"in_{n}": a for n, a in arrays.items()}], core_ids=[0])
    return r.results[0]["out_0"].reshape(BATCH, SEQ, D)
```

```python
from contextlib import ExitStack

import concourse.bass as bass
import numpy as np
from concourse import mybir

P = 128
BATCH, SEQ, D = 16, 256, 128
HEADS, HD = 16, 8
PAIRS = HEADS // 2
EXPERTS, HIDDEN, TOP_K = 8, 352, 2
TILES = BATCH * SEQ // P
HALVES = 2
TH = TILES // HALVES
NB = BATCH // HALVES
NT = TOP_K * TH + EXPERTS - 1
HC = -(-HIDDEN // P)
HP = HC * P
LN_EPS = 1e-5
FAR = 1e30
SIDE = PAIRS * (NB + 1 - 2)

RG = TH // 4
RING = 4
NTERM = 7
STACK = 2 * HD * NTERM

F32, BF16, I32 = mybir.dt.float32, mybir.dt.bfloat16, mybir.dt.int32
ALU, ACT, AX = mybir.AluOpType, mybir.ActivationFunctionType, mybir.AxisListType

C_ID, C_BEFORE, C_ONES = 0, P, 2 * P
C_REV = 3 * P
C_STEP = C_REV + EXPERTS
C_TILE = C_STEP + TH
C_SEG = C_TILE + NT
C_END = C_SEG + EXPERTS * TH


def constants():
    c = np.zeros((P, C_END), np.float32)
    c[:, C_ID:C_ID + P] = np.eye(P)
    c[:, C_BEFORE:C_BEFORE + P] = np.triu(np.ones((P, P)), 1)
    c[:, C_ONES:C_ONES + P] = 1
    c[:, C_REV:C_STEP] = EXPERTS - np.arange(EXPERTS)
    c[:, C_STEP:C_TILE] = P * np.arange(TH)
    c[:, C_TILE:C_SEG] = np.arange(NT)
    c[:, C_SEG:] = np.tile(np.arange(TH) > 0, EXPERTS)
    return c


def wait(eng, sem, value):
    if value > 0:
        eng.wait_ge(sem, value)


def steps(first, last, body, unroll):
    for i in range(first, last):
        body(i, i % unroll, i // unroll)


def advance(side, ticks, i):
    for _ in range(ticks(i)):
        next(side, None)


def one(view, i):
    return view[:, bass.ds(i, 1)].squeeze(1)


def build(nc, x, wq, wk, wv, wo, gate, bias, w1, w2, w3, consts, out):
    with ExitStack() as ctx:
        def sb(name, shape, dt=F32):
            return ctx.enter_context(nc.sbuf_tensor(name, shape, dt))

        def sem(name):
            return ctx.enter_context(nc.semaphore(name))

        X = sb("X", [P, TILES, D])
        CT = sb("CT", [P, C_END])
        W1 = sb("W1", [P, EXPERTS, HIDDEN])
        W3 = sb("W3", [P, EXPERTS, HIDDEN])
        W2 = sb("W2", [P, EXPERTS, HC, D])
        GATE = sb("GATE", [P, EXPERTS])
        BIAS = sb("BIAS", [P, EXPERTS])
        ident = CT[:, C_ID:C_ID + P]
        ones = CT[:, C_ONES:C_ONES + P]

        stats6 = sb("stats6", [P, TH, 6])
        mean, var, rstd, rough = ([sb(f"{n}{h}", [P, TH]) for h in range(HALVES)]
                                  for n in ("mean", "var", "rstd", "rough"))
        amean, arstd = sb("amean", [P, TILES]), sb("arstd", [P, TILES])
        msum, mdiff, msq, rr = (sb(n, [P, TH]) for n in ("msum", "mdiff", "msq", "rr"))
        half_power = sb("half_power", [P, TH])

        xr = sb("xr", [P, 8, D])
        xrT = sb("xrT", [P, 4, P])
        logits = sb("logits", [P, TH, EXPERTS])
        te3 = [P, TH, EXPERTS]
        shifted, weight, score = sb("shifted", te3), sb("weight", te3), sb("score", te3)
        biased, found = sb("biased", te3), sb("found", te3)
        chosen = sb("chosen", [P, TOP_K, TH, EXPERTS])
        picked = sb("picked", [P, TOP_K, TH, EXPERTS])
        colmax, total = sb("colmax", [P, TH]), sb("total", [P, TH])
        coef = sb("coef", [P, TOP_K, TH])
        et3 = [P, EXPERTS, TH]
        taken, upto, place = sb("taken", et3), sb("upto", et3), sb("place", et3)
        rowsum = sb("rowsum", [P, EXPERTS])
        tiles_of, last_tile, start = (sb(n, [P, EXPERTS]) for n in ("tiles_of", "last_tile", "start"))
        over = sb("over", [P, EXPERTS, TH])
        passed = sb("passed", [P, NT, EXPERTS])
        slot_f = sb("slot_f", [P, TOP_K, TH])
        slot = [sb(f"slot{h}", [P, TOP_K, TH], I32) for h in range(HALVES)]
        expert_f = sb("expert_f", [P, NT])
        expert = [sb(f"expert{h}", [P, NT], I32) for h in range(HALVES)]
        rows = [sb(f"rows{h}", [P, TOP_K, TH, D]) for h in range(HALVES)]

        xe = sb("xe", [P, RING, D])
        xeT = sb("xeT", [P, 2, P])
        act1 = sb("act1", [P, 2, HIDDEN])
        hid = sb("hid", [P, 2, HP])
        hidT = sb("hidT", [P, 2, HP])
        ye = sb("ye", [P, RING, D])
        zeros = sb("zeros", [P, NT * 32])

        slots_in = [nc.dram_tensor(f"slots_in{h}", [NT * P, D], F32).ap() for h in range(HALVES)]
        slots_out = [nc.dram_tensor(f"slots_out{h}", [NT * P, D], F32).ap() for h in range(HALVES)]

        WQ, WK, WV, WO = (sb(n, [P, D]) for n in ("WQ", "WK", "WV", "WO"))
        identb = sb("identb", [P, P], BF16)
        xa, xaT = sb("xa", [P, 2, D]), sb("xaT", [P, SEQ])
        split = sb("split", [P, 2, 3, SEQ], BF16)
        resid = sb("resid", [P, 2, SEQ])
        QS = [sb(f"QS{q}", [P, PAIRS, 2, SEQ], BF16) for q in range(2)]
        KS = [sb(f"KS{q}", [P, PAIRS, SEQ], BF16) for q in range(2)]
        zrows = sb("zrows", [2, 4 * 2 * SEQ], BF16)
        V1 = [sb(f"V1_{q}", [P, 2, HEADS, 32]) for q in range(4)]
        PT = sb("PT", [P, 4, 2, SEQ])
        mx = sb("mx", [P, 2, PAIRS, 2])
        nm = sb("nm", [P, 2, 4 * PAIRS], BF16)
        nmT = sb("nmT", [4 * PAIRS, SEQ], BF16)
        oT = sb("oT", [P, HEADS // 4, SEQ])
        rsum, on = sb("rsum", [P, 2, HEADS]), sb("on", [P, 2, D])
        onT = sb("onT", [P, SEQ])
        scratch = nc.dram_tensor("stacks", [2, 2, 2, PAIRS, HD, NTERM, SEQ], BF16).ap()

        banks = ctx.enter_context(nc.psum_tensor("banks", [P, 8, 512], F32))
        PS = [banks[:, b, :] for b in range(8)]

        s_x = [sem(f"s_x{h}") for h in range(HALVES)]
        s_const = sem("s_const")
        s_w = sem("s_w")
        s_cleared = [sem(f"s_cleared{h}") for h in range(HALVES)]
        s_zero = sem("s_zero")
        s_dve = sem("s_dve")
        s_var, s_pow = sem("s_var"), sem("s_pow")
        s_xr, s_rt, s_rte, s_lg = sem("s_xr"), sem("s_rt"), sem("s_rte"), sem("s_lg")
        s_shift, s_exp = sem("s_shift"), sem("s_exp")
        s_rowsum, s_count = sem("s_rowsum"), sem("s_count")
        s_slot, s_rows, s_expert, s_lgread = sem("s_slot"), sem("s_rows"), sem("s_expert"), sem("s_lgread")
        s_scat = [sem(f"s_scat{h}") for h in range(HALVES)]
        s_xe = [sem(f"s_xe{r}") for r in range(RING)]
        s_xt, s_xte, s_u1, s_u3 = sem("s_xt"), sem("s_xte"), sem("s_u1"), sem("s_u3")
        s_act, s_hid, s_ht, s_hte = sem("s_act"), sem("s_hid"), sem("s_ht"), sem("s_hte")
        s_y, s_ye = sem("s_y"), sem("s_ye")
        s_st = [sem(f"s_st{r}") for r in range(RING)]
        GC = 4
        s_gath = [[sem(f"s_gath{h}_{c}") for c in range(GC)] for h in range(HALVES)]
        s_comb = sem("s_comb")
        s_out = sem("s_out")
        s_xa, s_at, s_ate, s_qk, s_v, s_ve = (sem(n) for n in ("s_xa", "s_at", "s_ate", "s_qk", "s_v", "s_ve"))
        s_hi, s_res, s_mid, s_lo = (sem(n) for n in ("s_hi", "s_res", "s_mid", "s_lo"))
        s_wr = [sem(f"s_wr{q}") for q in range(2)]
        s_stack = [[sem(f"s_stack{q}_{c}") for c in range(2)] for q in range(2)]
        s_mrow = [sem(f"s_mrow{q}") for q in range(2)]
        s_s, s_max, s_nm, s_nmt, s_nmte = (sem(n) for n in ("s_s", "s_max", "s_nm", "s_nmt", "s_nmte"))
        s_sc, s_exp2, s_av, s_ove = (sem(n) for n in ("s_sc", "s_exp2", "s_av", "s_ove"))
        s_ot, s_on, s_ont, s_onte, s_proj, s_add = (sem(n) for n in ("s_ot", "s_on", "s_ont", "s_onte",
                                                                     "s_proj", "s_add"))
        s_wa, s_vzero = sem("s_wa"), sem("s_vzero")

        chain = [0]

        def link(eng, ins):
            chain[0] += 1
            ins.then_inc(s_dve, 1)
            eng.wait_ge(s_dve, chain[0])

        block = ctx.enter_context(nc.Block())

        def norm_stats(eng, h, tiles, mean):
            for t in range(0, TH, 4):
                for i in range(t, t + 4):
                    chain[0] += 1
                    eng.bn_stats(stats6[:, i, :], tiles[:, i, :]).then_inc(s_dve, 1)
                yield
            eng.wait_ge(s_dve, chain[0])
            link(eng, eng.tensor_tensor(msum[:], stats6[:, :, 1], stats6[:, :, 4], ALU.add))
            link(eng, eng.tensor_tensor(mdiff[:], stats6[:, :, 1], stats6[:, :, 4], ALU.subtract))
            link(eng, eng.tensor_tensor(var[h][:], stats6[:, :, 2], stats6[:, :, 5], ALU.add))
            yield
            link(eng, eng.tensor_scalar(mean, msum[:], 0.5, None, ALU.mult))
            link(eng, eng.scalar_tensor_tensor(msq[:], mdiff[:], 0.25, mdiff[:], ALU.mult, ALU.mult))
            link(eng, eng.tensor_scalar(var[h][:], var[h][:], 1.0 / D, LN_EPS, ALU.mult, ALU.add))
            eng.tensor_tensor(var[h][:], var[h][:], msq[:], ALU.add).then_inc(s_var, 1)
            yield

        def norm_root(eng, n, h, rstd):
            yield
            eng.wait_ge(s_pow, n + 1)
            link(eng, eng.tensor_tensor(rr[:], rough[h][:], rough[h][:], ALU.mult))
            link(eng, eng.scalar_tensor_tensor(rr[:], rr[:], -0.5, var[h][:], ALU.mult, ALU.mult))
            link(eng, eng.scalar_tensor_tensor(rstd, rr[:], 1.5, rough[h][:], ALU.add, ALU.mult))
            yield

        def norm_of_attention(eng, h, n):
            tiles = slice(h * TH, (h + 1) * TH)
            yield from norm_stats(eng, h, X[:, tiles, :], amean[:, tiles])
            yield from norm_root(eng, n, h, arstd[:, tiles])

        def route_norm(eng, n, h):
            yield from norm_stats(eng, h, X[:, h * TH:(h + 1) * TH, :], mean[h][:])
            yield from norm_root(eng, n, h, rstd[h][:])

        def route_vector(eng, g, h):
            xh = X[:, h * TH:(h + 1) * TH, :]

            def normed(k):
                wait(eng, s_rt, RG * g + k - 1)
                for i in range(4 * k, 4 * k + 4):
                    eng.tensor_scalar(xr[:, i % 8, :], xh[:, i, :], mean[h][:, i:i + 1], rstd[h][:, i:i + 1],
                                      ALU.subtract, ALU.mult).then_inc(s_xr, 1)

            normed(0)
            for k in range(RG):
                if k:
                    eng.wait_ge(s_lg, RG * g + k)
                    eng.tensor_copy(logits[:, 4 * k - 4:4 * k, :],
                                    PS[7][:, 0:4 * EXPERTS].rearrange("p (t e) -> p t e", e=EXPERTS))\
                       .then_inc(s_lgread, 1)
                if k + 1 < RG:
                    normed(k + 1)
                for _ in range(6):
                    yield
            eng.wait_ge(s_lg, RG * (g + 1))
            eng.tensor_copy(logits[:, TH - 4:TH, :],
                            PS[7][:, 0:4 * EXPERTS].rearrange("p (t e) -> p t e", e=EXPERTS))\
               .then_inc(s_lgread, 1)
            eng.wait_ge(s_lgread, (RG + 1) * g + RG)
            over_e = lambda a: a.unsqueeze(2).to_broadcast([P, TH, EXPERTS])
            over_t = lambda a: a.unsqueeze(1).to_broadcast([P, TH, EXPERTS])
            rev = over_t(CT[:, C_REV:C_STEP])
            link(eng, eng.tensor_reduce(colmax[:], logits[:], AX.X, ALU.max))
            yield
            eng.tensor_tensor(shifted[:], logits[:], over_e(colmax[:, :]), ALU.subtract).then_inc(s_shift, 1)
            yield
            yield
            yield
            eng.wait_ge(s_exp, g + 1)
            link(eng, eng.tensor_reduce(total[:], weight[:], AX.X, ALU.add))
            link(eng, eng.reciprocal(total[:], total[:]))
            yield
            link(eng, eng.tensor_tensor(score[:], weight[:], over_e(total[:, :]), ALU.mult))
            link(eng, eng.tensor_tensor(biased[:], score[:], over_t(BIAS[:, :]), ALU.add))
            yield
            for k in range(TOP_K):
                link(eng, eng.tensor_reduce(colmax[:], biased[:], AX.X, ALU.max))
                link(eng, eng.tensor_tensor(found[:], biased[:], over_e(colmax[:, :]), ALU.is_equal))
                yield
                link(eng, eng.tensor_tensor(found[:], found[:], rev, ALU.mult))
                link(eng, eng.tensor_reduce(colmax[:], found[:], AX.X, ALU.max))
                yield
                link(eng, eng.tensor_tensor(chosen[:, k], rev, over_e(colmax[:, :]), ALU.is_equal))
                if k + 1 < TOP_K:
                    link(eng, eng.scalar_tensor_tensor(biased[:], chosen[:, k], -FAR, biased[:],
                                                       ALU.mult, ALU.add))
                yield
            link(eng, eng.tensor_tensor(taken[:].rearrange("p e t -> p t e"), chosen[:, 0], chosen[:, 1],
                                        ALU.add))
            eng.tensor_reduce(rowsum[:], taken[:], AX.X, ALU.add).then_inc(s_rowsum, 1)
            yield
            for k in range(TOP_K):
                link(eng, eng.tensor_tensor(picked[:, k], chosen[:, k], score[:], ALU.mult))
            yield
            link(eng, eng.tensor_reduce(coef[:], picked[:], AX.X, ALU.add))
            for k in range(TOP_K):
                link(eng, eng.tensor_tensor(coef[:, k], coef[:, k], rstd[h][:], ALU.mult))
            yield
            flat = lambda a: a[:].rearrange("p e t -> p (e t)")
            link(eng, eng.tensor_tensor_scan(flat(upto), CT[:, C_SEG:C_END], flat(taken), 0.0,
                                             ALU.mult, ALU.add))
            link(eng, eng.tensor_tensor(place[:], upto[:], taken[:], ALU.subtract))
            yield
            eng.wait_ge(s_count, g + 1)
            before, counts = PS[7][:, 0:EXPERTS], PS[7][:, EXPERTS:2 * EXPERTS]
            et = [P, EXPERTS, TH]
            link(eng, eng.tensor_tensor(over[:], counts.unsqueeze(2).to_broadcast(et),
                                        CT[:, C_STEP:C_TILE].unsqueeze(1).to_broadcast(et), ALU.is_gt))
            link(eng, eng.tensor_reduce(tiles_of[:], over[:], AX.X, ALU.add))
            yield
            link(eng, eng.tensor_tensor_scan(last_tile[:], CT[:, C_ONES:C_ONES + EXPERTS], tiles_of[:],
                                             0.0, ALU.mult, ALU.add))
            link(eng, eng.tensor_tensor(start[:], last_tile[:], tiles_of[:], ALU.subtract))
            eng.scalar_tensor_tensor(start[:], start[:], float(P), before, ALU.mult, ALU.add).then_inc(s_lgread, 1)
            eng.wait_ge(s_lgread, (RG + 1) * (g + 1))
            yield
            link(eng, eng.tensor_tensor(place[:], place[:], start[:, :].unsqueeze(2).to_broadcast(et), ALU.add))
            for k in range(TOP_K):
                link(eng, eng.tensor_tensor(picked[:, k], chosen[:, k],
                                            place[:].rearrange("p e t -> p t e"), ALU.mult))
            yield
            link(eng, eng.tensor_reduce(slot_f[:], picked[:], AX.X, ALU.add))
            eng.tensor_copy(slot[h][:], slot_f[:]).then_inc(s_slot, 1)
            yield
            for k in range(TOP_K):
                for i in range(TH):
                    eng.tensor_scalar(rows[h][:, k, i, :], xh[:, i, :], mean[h][:, i:i + 1],
                                      coef[:, k, i:i + 1], ALU.subtract, ALU.mult).then_inc(s_rows, 1)
                    if i % 4 == 3:
                        yield
            ne = [P, NT, EXPERTS]
            link(eng, eng.tensor_tensor(passed[:], CT[:, C_TILE:C_SEG].unsqueeze(2).to_broadcast(ne),
                                        last_tile[:, :].unsqueeze(1).to_broadcast(ne), ALU.is_ge))
            yield
            link(eng, eng.tensor_reduce(expert_f[:], passed[:], AX.X, ALU.add))
            link(eng, eng.tensor_scalar(expert_f[:], expert_f[:], float(EXPERTS - 1), None, ALU.min))
            eng.tensor_copy(expert[h][:], expert_f[:]).then_inc(s_expert, 1)
            yield

        def route_tensor(eng, g):
            for _ in range(10):
                yield
            for k in range(RG):
                eng.wait_ge(s_xr, TH * g + 4 * k + 4)
                wait(eng, s_lgread, (RG + 1) * g + k)
                for i in range(4):
                    last = eng.transpose(PS[7][:, i * P:(i + 1) * P], xr[:, 4 * (k % 2) + i, :], ident)
                last.then_inc(s_rt, 1)
                yield
                yield
                eng.wait_ge(s_rte, RG * g + k + 1)
                for i in range(4):
                    last = eng.matmul(PS[7][:, i * EXPERTS:(i + 1) * EXPERTS], xrT[:, i, :], GATE[:],
                                      start=True, stop=True)
                last.then_inc(s_lg, 1)
                for _ in range(4):
                    yield
            for _ in range(12):
                yield
            eng.wait_ge(s_rowsum, g + 1)
            eng.matmul(PS[7][:, 0:EXPERTS], CT[:, C_BEFORE:C_BEFORE + P], rowsum[:], start=True, stop=True)
            eng.matmul(PS[7][:, EXPERTS:2 * EXPERTS], ones, rowsum[:], start=True, stop=True)\
               .then_inc(s_count, 1)
            yield

        def route_scalar(eng, g):
            for _ in range(11):
                yield
            for k in range(RG):
                eng.wait_ge(s_rt, RG * g + k + 1)
                wait(eng, s_lg, RG * g + k)
                eng.copy(xrT[:].rearrange("p t n -> p (t n)"), PS[7]).then_inc(s_rte, 1)
                for _ in range(6 if k + 1 < RG else 5):
                    yield
            eng.wait_ge(s_shift, g + 1)
            eng.activation(weight[:], shifted[:], ACT.Exp).then_inc(s_exp, 1)
            yield

        def root_gpsimd(eng, n):
            eng.wait_ge(s_var, n + 1)
            eng.tensor_tensor(rough[n % 2][:], var[n % 2][:], half_power[:], ALU.pow).then_inc(s_pow, 1)

        def scatter_gpsimd(eng, g, h):
            if g < HALVES:
                eng.wait_ge(s_cleared[h], 16)
            eng.wait_ge(s_slot, g + 1)
            for k in range(TOP_K):
                for t in range(TH):
                    if t % 4 == 0:
                        eng.wait_ge(s_rows, (TOP_K * g + k) * TH + t + 4)
                    eng.indirect_dma_start(slots_in[h], bass.IndirectOffsetOnAxis(ap=slot[h][:, k, t:t + 1], axis=0),
                                           rows[h][:, k, t, :], None).then_inc(s_scat[h], 16)

        def gather_gpsimd(eng, g, h):
            for r in range(RING):
                eng.wait_ge(s_st[r], 16 * stored(g + 1, r))
            per = TH // GC
            for c in range(GC):
                for t in range(c * per, (c + 1) * per):
                    for k in range(TOP_K):
                        eng.indirect_dma_start(rows[h][:, k, t, :], None, slots_out[h],
                                               bass.IndirectOffsetOnAxis(ap=slot[h][:, k, t:t + 1], axis=0))\
                           .then_inc(s_gath[h][c], 16)

        def combine_vector(eng, g, h):
            per = TH // GC
            for c in range(GC):
                eng.wait_ge(s_gath[h][c], 16 * TOP_K * per * (g // HALVES + 1))
                a, b = (rows[h][:, k, c * per:(c + 1) * per, :] for k in range(TOP_K))
                xc = X[:, h * TH + c * per:h * TH + (c + 1) * per, :]
                link(eng, eng.tensor_tensor(a, a, b, ALU.add))
                yield
                eng.scalar_tensor_tensor(xc, a, 0.5, xc, ALU.mult, ALU.add).then_inc(s_comb, 1)
                yield
            eng.wait_ge(s_comb, GC * (g + 1))

        def stored(g, r):
            return g * len(range(r, NT, RING))

        def expert_sync(eng, g, h):
            b = g * NT
            eng.wait_ge(s_scat[h], 16 * TOP_K * TH * (g // HALVES + 1))
            lag = RING + 2

            def body(i, r, j):
                if i < NT:
                    wait(eng, s_xt, b + i - RING + 1)
                    eng.dma_start(xe[:, r, :], slots_in[h][bass.ds(i * P, P), :]).then_inc(s_xe[r], 16)
                if i >= lag:
                    eng.wait_ge(s_ye, b + i - lag + 1)
                    q = (r - lag) % RING
                    eng.dma_start(slots_out[h][bass.ds((i - lag) * P, P), :], ye[:, q, :]).then_inc(s_st[q], 16)

            steps(0, NT + lag, body, RING)

        def expert_tensor(eng, g, h, side, ticks):
            b = g * NT

            def number(i):
                return eng.value_load(expert[h][0:1, bass.ds(i, 1)], min_val=0, max_val=EXPERTS - 1)

            def turn(i, r, j):
                eng.wait_ge(s_xe[r], 16 * (stored(g, r) + 1 + j))
                wait(eng, s_xte, b + i)
                eng.transpose(PS[0][:, 0:P], xe[:, r, :], ident).then_inc(s_xt, 1)

            def up(i, r):
                e = number(i)
                eng.wait_ge(s_xte, b + i + 1)
                wait(eng, s_act, b + i - 1)
                eng.matmul(PS[2 + r][:, 0:HIDDEN], xeT[:, r, :], one(W1[:, :, :], e), start=True, stop=True)\
                   .then_inc(s_u1, 1)
                wait(eng, s_hid, b + i - 1)
                eng.matmul(PS[4 + r][:, 0:HIDDEN], xeT[:, r, :], one(W3[:, :, :], e), start=True, stop=True)\
                   .then_inc(s_u3, 1)

            def down(i, r):
                e = number(i)
                eng.wait_ge(s_hte, b + i + 1)
                wait(eng, s_ye, b + i)
                for c in range(HC):
                    last = eng.matmul(PS[1][:, 0:D], hidT[:, r, c * P:(c + 1) * P], one(W2[:, :, c, :], e),
                                      start=c == 0, stop=c == HC - 1)
                last.then_inc(s_y, 1)

            def turn_hidden(i, r):
                eng.wait_ge(s_hid, b + i + 1)
                wait(eng, s_hte, b + i)
                for c in range(HC):
                    last = eng.transpose(PS[6][:, c * P:(c + 1) * P], hid[:, r, c * P:(c + 1) * P], ident)
                last.then_inc(s_ht, 1)

            def body(i, r, j):
                if -1 <= i < NT - 1:
                    turn(i + 1, (r + 1) % RING, j + (r + 1) // RING)
                if 0 <= i < NT:
                    up(i, r % 2)
                if 2 <= i:
                    down(i - 2, r % 2)
                if 1 <= i <= NT:
                    turn_hidden(i - 1, 1 - r % 2)
                advance(side, ticks, i)

            if g == 0:
                eng.wait_ge(s_w, 16 * (3 + EXPERTS))
            eng.wait_ge(s_expert, g + 1)
            steps(-1, NT + 2, body, RING)

        def expert_scalar(eng, g, side, ticks):
            b = g * NT

            def body(i, r, j):
                if -1 <= i < NT - 1:
                    eng.wait_ge(s_xt, b + i + 2)
                    wait(eng, s_u3, b + i)
                    eng.copy(xeT[:, 1 - r % 2, :], PS[0][:, 0:P]).then_inc(s_xte, 1)
                if 0 <= i < NT:
                    eng.wait_ge(s_u1, b + i + 1)
                    wait(eng, s_hid, b + i - 1)
                    eng.activation(act1[:, r % 2, :], PS[2 + r % 2][:, 0:HIDDEN], ACT.Silu).then_inc(s_act, 1)
                if 2 <= i:
                    q, before = (r - 2) % RING, j + (r - 2) // RING
                    eng.wait_ge(s_y, b + i - 1)
                    wait(eng, s_st[q], 16 * (stored(g, q) + before))
                    eng.copy(ye[:, q, :], PS[1][:, 0:D]).then_inc(s_ye, 1)
                advance(side, ticks, i)

            steps(-1, NT + 2, body, RING)

        def expert_vector(eng, g, side, ticks):
            b = g * NT

            def body(i, r, j):
                if i < NT:
                    eng.wait_ge(s_act, b + i + 1)
                    eng.wait_ge(s_u3, b + i + 1)
                    wait(eng, s_ht, b + i - 1)
                    eng.tensor_tensor(hid[:, r % 2, 0:HIDDEN], PS[4 + r % 2][:, 0:HIDDEN], act1[:, r % 2, :], ALU.mult)\
                       .then_inc(s_hid, 1)
                if i >= 1:
                    eng.wait_ge(s_ht, b + i)
                    wait(eng, s_y, b + i - 2)
                    eng.tensor_copy(hidT[:, 1 - r % 2, :], PS[6][:, 0:HP]).then_inc(s_hte, 1)
                advance(side, ticks, i)

            steps(0, NT + 1, body, RING)

        FILLS = ((4, 6), (6, 8), (8, 11), (11, 14), (14, 16), (), (0, 2), (2, 4))
        scale = float(HD) ** -0.5

        def fills(n, u):
            m = n + 1 + (u >= 6)
            return [(m, f, f // 2, f % 2) for f in range(*FILLS[u])] if FILLS[u] and 0 <= m < BATCH else []

        def attention_tensor(eng, side, ticks):
            for n in range(-3, BATCH + 1):
                ahead, nxt, now, done = (0 <= n + 3 < BATCH, 0 <= n + 1 < BATCH, 0 <= n < BATCH, 0 <= n - 1 < BATCH)
                for u in range(PAIRS):
                    fill = maxima_scores(eng, fills(n, u))
                    next(fill, None)
                    if now:
                        q = n % 2
                        if u == 0:
                            eng.wait_ge(s_mrow[q], 32 * (n // 2 + 1))
                        for kt in range(2):
                            f = 2 * (PAIRS * n + u) + kt
                            wait(eng, s_exp2, f - 2)
                            eng.matmul(PS[f % 3], KS[q][:, u, kt * P:(kt + 1) * P],
                                       QS[q][:, u, :, :].rearrange("p e n -> p (e n)"),
                                       start=True, stop=True).then_inc(s_sc, 1)
                    next(fill, None)
                    if now and u > 0:
                        values(eng, n, u - 1)
                    next(fill, None)
                    if ahead and u == 0:
                        m = n + 3
                        eng.wait_ge(s_xa, 2 * (m + 1))
                        wait(eng, s_ve, m)
                        wait(eng, s_nmte, n + 1)
                        wait(eng, s_add, n - 1)
                        for i in range(2):
                            last = eng.transpose(PS[6][:, i * P:(i + 1) * P], xa[:, i, :], ident)
                        last.then_inc(s_at, 1)
                    if ahead and u == 1:
                        eng.wait_ge(s_ate, n + 4)
                        for part, w in enumerate((WQ, WK)):
                            last = eng.matmul(PS[6][:, part * SEQ:(part + 1) * SEQ], w[:], xaT[:],
                                              start=True, stop=True)
                        last.then_inc(s_qk, 1)
                    if ahead and u == 2:
                        eng.wait_ge(s_res, n + 4)
                        for kt in range(2):
                            last = eng.matmul(PS[6][:, kt * P:(kt + 1) * P], xaT[:, kt * P:(kt + 1) * P], WV[:],
                                              start=True, stop=True)
                        last.then_inc(s_v, 1)
                    if done and u in (3, 4):
                        qt = u - 3
                        eng.wait_ge(s_ove, 2 * n)
                        if u == 3:
                            eng.wait_ge(s_ve, min(n + 4, BATCH))
                            eng.wait_ge(s_nmte, min(n + 1, BATCH))
                            wait(eng, s_add, n - 1)
                        else:
                            eng.wait_ge(s_on, 2 * n - 1)
                        for c in range(HEADS // 4):
                            last = eng.transpose(PS[6][:, c * P:(c + 1) * P], oT[:, c, qt * P:(qt + 1) * P], ident)
                        last.then_inc(s_ot, 1)
                    if done and u == 6:
                        eng.wait_ge(s_on, 2 * n)
                        if nxt:
                            eng.wait_ge(s_nmte, n + 2)
                        for qt in range(2):
                            last = eng.transpose(PS[6][:, qt * P:(qt + 1) * P], on[:, qt, :], ident)
                        last.then_inc(s_ont, 1)
                    if nxt and u == 5:
                        eng.wait_ge(s_nm, n + 2)
                        if done:
                            eng.wait_ge(s_on, 2 * n)
                        elif ahead:
                            eng.wait_ge(s_ve, n + 4)
                        for qt in range(2):
                            last = eng.transpose(PS[6][0:4 * PAIRS, :].bitcast(BF16)[:, qt * P:(qt + 1) * P],
                                                 nm[:, qt, :], identb[:])
                        last.then_inc(s_nmt, 1)
                    if done and u == 7:
                        eng.wait_ge(s_onte, n)
                        for qt in range(2):
                            last = eng.matmul(PS[6][:, qt * P:(qt + 1) * P], onT[:, qt * P:(qt + 1) * P], WO[:],
                                              start=True, stop=True)
                        last.then_inc(s_proj, 1)
                    if now and u == PAIRS - 1:
                        values(eng, n, u)
                    advance(side, ticks, PAIRS * n + u)

        def maxima_scores(eng, todo):
            for m, f, pair, qt in todo:
                q = m % 2
                if f % 8 == 0:
                    eng.wait_ge(s_stack[q][f // 8], 80 * (m // 2 + 1))
                wait(eng, s_max, 2 * PAIRS * m + f - 1)
                for e in range(2):
                    last = eng.matmul(PS[3 + f % 2][:, e * SEQ:(e + 1) * SEQ],
                                      QS[q][:, pair, e, qt * P:(qt + 1) * P], KS[q][:, pair, :],
                                      start=True, stop=True)
                last.then_inc(s_s, 1)
                yield

        def values(eng, n, u):
            eng.wait_ge(s_exp2, 2 * (PAIRS * n + u + 1))
            if u == 0:
                eng.wait_ge(s_ve, n + 1)
            if u % 4 == 0:
                wait(eng, s_ove, 2 * n + u // 4)
            for e in range(2):
                j = (2 * u + e) % 4
                for kt in range(2):
                    last = eng.matmul(PS[5][32 * j:32 * j + 32, (u // 2 % 2) * SEQ:(u // 2 % 2 + 1) * SEQ],
                                      V1[n % 4][:, kt, 2 * u + e, :], PT[:, 2 * (u % 2) + kt, e, :],
                                      start=kt == 0, stop=kt == 1, tile_position=(0, 32 * j))
            last.then_inc(s_av, 1)

        def attention_scalar(eng, side, ticks):
            for n in range(-3, BATCH + 1):
                ahead, nxt, now, done = (0 <= n + 3 < BATCH, 0 <= n + 1 < BATCH, 0 <= n < BATCH, 0 <= n - 1 < BATCH)
                for u in range(PAIRS):
                    if now:
                        wait(eng, s_av, PAIRS * n + u - 1)
                        for kt in range(2):
                            f = 2 * (PAIRS * n + u) + kt
                            eng.wait_ge(s_sc, f + 1)
                            eng.activation(PT[:, f % 4].rearrange("p e n -> p (e n)"), PS[f % 3], ACT.Exp,
                                           scale=scale).then_inc(s_exp2, 1)
                    if u == 0 and done:
                        read_values(eng, n - 1, 1)
                    if u == 4 and now:
                        read_values(eng, n, 0)
                    if u == 0 and ahead:
                        eng.wait_ge(s_at, n + 4)
                        wait(eng, s_v, n + 3)
                        eng.copy(xaT[:], PS[6][:, 0:SEQ]).then_inc(s_ate, 1)
                    if u == 1 and ahead:
                        eng.wait_ge(s_qk, n + 4)
                        if n + 2 >= 0:
                            eng.wait_ge(s_wr[n % 2], 64 * ((n + 2) // 2 + 1))
                        eng.copy(split[:, :, 0, :], PS[6][:, :].rearrange("p (s n) -> p s n", s=2)).then_inc(s_hi, 1)
                    if u == 2 and ahead:
                        eng.wait_ge(s_res, n + 4)
                        eng.copy(split[:, :, 1, :], resid[:, :, :]).then_inc(s_mid, 1)
                        q = (n + 3) % 4
                        eng.wait_ge(s_v, n + 4)
                        wait(eng, s_av, PAIRS * n)
                        eng.copy(V1[q][:, :, :, 0:HD],
                                 PS[6][:, 0:2 * P].rearrange("p (k a d) -> p k a d", k=2, d=HD)).then_inc(s_ve, 1)
                    if u == 6 and done:
                        eng.wait_ge(s_ont, n)
                        wait(eng, s_proj, n - 1)
                        eng.copy(onT[:], PS[6][:, 0:SEQ]).then_inc(s_onte, 1)
                    if u == 5 and nxt:
                        eng.wait_ge(s_nmt, n + 2)
                        if n + 1 > 0:
                            p = n % 2
                            eng.wait_ge(s_mrow[p], 32 * (n // 2 + 1))
                        eng.copy(nmT[:], PS[6][0:4 * PAIRS, :].bitcast(BF16)[:, 0:SEQ]).then_inc(s_nmte, 1)
                    advance(side, ticks, PAIRS * n + u)

        def read_values(eng, n, i):
            eng.wait_ge(s_av, PAIRS * n + 4 * (i + 1))
            wait(eng, s_ot, 2 * n)
            eng.copy(oT[:, 2 * i:2 * i + 2, :].rearrange("p c n -> p (c n)"), PS[5][:, :]).then_inc(s_ove, 1)

        def normed_pair(eng, n):
            wait(eng, s_at, n)
            for i in range(2):
                t = 2 * n + i
                eng.tensor_scalar(xa[:, i, :], X[:, t, :], amean[:, t:t + 1], arstd[:, t:t + 1],
                                  ALU.subtract, ALU.mult).then_inc(s_xa, 1)

        def attention_vector(eng, side, ticks):
            normed_pair(eng, 0)
            for n in range(-3, BATCH + 1):
                ahead, nxt, now, done = (0 <= n + 3 < BATCH, 0 <= n + 1 < BATCH, 0 <= n < BATCH, 0 <= n - 1 < BATCH)
                for u in range(PAIRS):
                    if u == 2 and ahead:
                        eng.wait_ge(s_hi, n + 4)
                        eng.tensor_tensor(resid[:], PS[6][:, :].rearrange("p (s n) -> p s n", s=2),
                                          split[:, :, 0, :], ALU.subtract).then_inc(s_res, 1)
                    for m, f, pair, qt in fills(n, u):
                        eng.wait_ge(s_s, 2 * PAIRS * m + f + 1)
                        if f == 0:
                            wait(eng, s_nm, m)
                        eng.tensor_reduce(mx[:, qt, pair, :], PS[3 + f % 2][:, :].rearrange("p (e n) -> p e n", e=2),
                                          AX.X, ALU.max).then_inc(s_max, 1)
                    if u == 2 and ahead:
                        eng.wait_ge(s_mid, n + 4)
                        eng.tensor_tensor(split[:, :, 2, :], resid[:], split[:, :, 1, :], ALU.subtract).then_inc(s_lo, 1)
                    if u in (3, 4) and done:
                        qt = u - 3
                        eng.wait_ge(s_ot, 2 * n - 1 + qt)
                        sums = PS[6][:, :].rearrange("p (a c) -> p a c", c=32)
                        link(eng, eng.reciprocal(rsum[:, qt, :], sums[:, :, HD]))
                        wait(eng, s_ont, n - 1)
                        eng.tensor_tensor(on[:, qt, :].rearrange("p (a d) -> p a d", d=HD), sums[:, :, 0:HD],
                                          rsum[:, qt, :].unsqueeze(2).to_broadcast([P, HEADS, HD]),
                                          ALU.mult).then_inc(s_on, 1)
                    if u == 4 and nxt:
                        eng.wait_ge(s_max, 2 * PAIRS * (n + 2))
                        wait(eng, s_nmt, n + 1)
                        m4 = mx[:].rearrange("p q r e -> p q (r e)")
                        n4 = nm[:].rearrange("p q (t m) -> p q t m", t=2)
                        link(eng, eng.tensor_scalar(n4[:, :, 0, :], m4, -1.0, None, ALU.mult))
                        eng.scalar_tensor_tensor(n4[:, :, 1, :], m4, -1.0, n4[:, :, 0, :], ALU.mult,
                                                 ALU.subtract).then_inc(s_nm, 1)
                    if u == 6 and 0 <= n + 4 < BATCH:
                        normed_pair(eng, n + 4)
                    if u == 7 and done:
                        eng.wait_ge(s_proj, n)
                        xb = X[:, 2 * n - 2:2 * n, :]
                        eng.tensor_tensor(xb, PS[6][:, 0:SEQ].rearrange("p (q n) -> p q n", q=2), xb,
                                          ALU.add).then_inc(s_add, 1)
                    advance(side, ticks, PAIRS * n + u)

        def attention_sync(eng):
            for n in range(-3, BATCH):
                if n < 0 <= n + 2:
                    stack(eng, n, n + 2, 0)
                    stack(eng, n, n + 2, 1)
                if n + 3 < BATCH:
                    m, q = n + 3, (n + 3) % 2
                    eng.wait_ge(s_lo, m + 1)
                    if m >= 2:
                        for c in range(2):
                            eng.wait_ge(s_stack[q][c], 80 * (m // 2))
                    flat = scratch[q].rearrange("s e r d t n -> s (e r d) t n")
                    for s, reps in ((0, 2), (1, 3)):
                        parts = 6 // reps
                        eng.dma_start(flat[s, :, 0:6, :].rearrange("c (a b) n -> c a (b n)", a=reps),
                                      split[:, s, 0:parts, :].rearrange("c b n -> c (b n)").unsqueeze(1)
                                      .to_broadcast([P, reps, parts * SEQ])).then_inc(s_wr[q], 16)
                    eng.dma_start(flat[0, :, 6, :], split[:, 0, 0, :]).then_inc(s_wr[q], 16)
                    eng.dma_start(flat[1, :, 6, :], split[:, 1, 2, :]).then_inc(s_wr[q], 16)
                if n >= 0 and n + 2 < BATCH:
                    stack(eng, n, n + 2, 0)
                if 0 <= n + 1 < BATCH:
                    m, q = n + 1, (n + 1) % 2
                    eng.wait_ge(s_nmte, m + 1)
                    for t in range(2):
                        eng.dma_start(QS[q][STACK + t:STACK + t + 1].rearrange("p r e n -> p (r e) n"),
                                      nmT[2 * PAIRS * t:2 * PAIRS * (t + 1), :]).then_inc(s_mrow[q], 16)
                if n >= 0 and n + 2 < BATCH:
                    stack(eng, n, n + 2, 1)

        def stack(eng, n, m, c):
            q = m % 2
            eng.wait_ge(s_wr[q], 64 * (m // 2 + 1))
            wait(eng, s_sc, 2 * (PAIRS * n + 4 * (c + 1)))
            pairs = slice(4 * c, 4 * c + 4)
            for e in range(2):
                for side, dst in ((0, QS[q][:, pairs, e, :]), (1, KS[q][:, pairs, :])):
                    eng.dma_start(dst[e * STACK // 2:(e + 1) * STACK // 2],
                                  scratch[q, side, e, pairs].rearrange("r d t n -> (d t) r n"))\
                       .then_inc(s_stack[q][c], 16)
            eng.dma_start(QS[q][STACK:STACK + 2, pairs, :, :].rearrange("p r e n -> p (r e n)"), zrows[:])\
               .then_inc(s_stack[q][c], 16)


        @block.sync
        def _(sp):
            xv = x.rearrange("(t p) d -> p t d", p=P)
            sp.dma_start(CT[:], consts).then_inc(s_const, 16)
            sp.dma_start(X[:, 0:TH, :], xv[:, 0:TH, :]).then_inc(s_x[0], 16)
            sp.dma_start(GATE[:], gate).then_inc(s_const, 16)
            sp.dma_start(BIAS[:], bias.partition_broadcast(P)).then_inc(s_const, 16)
            sp.dma_start(X[:, TH:TILES, :], xv[:, TH:TILES, :]).then_inc(s_x[1], 16)
            sp.wait_ge(s_zero, 1)
            for h in range(HALVES):
                sp.dma_start(slots_in[h].rearrange("(p r) d -> p (r d)", p=P).rearrange("p (a n) -> p a n", a=4),
                             zeros[:, :].unsqueeze(1).to_broadcast([P, 4, NT * 32])).then_inc(s_cleared[h], 16)
            sp.dma_start(W1[:], w1.rearrange("e d h -> d e h")).then_inc(s_w, 16)
            sp.dma_start(W3[:], w3.rearrange("e d h -> d e h")).then_inc(s_w, 16)
            full = HIDDEN // P * P
            for e in range(EXPERTS):
                sp.dma_start(W2[:, e, 0:HC - 1, :], w2[e, 0:full, :].rearrange("(c p) d -> p c d", p=P))\
                  .then_inc(s_w, 16)
            sp.wait_ge(s_zero, 4)
            sp.dma_start(W2[0:HIDDEN - full, :, HC - 1, :], w2[:, full:HIDDEN, :].rearrange("e p d -> p e d"))\
              .then_inc(s_w, 16)
            for w, a in ((WQ, wq), (WK, wk), (WV, wv), (WO, wo)):
                sp.dma_start(w[:], a).then_inc(s_wa, 16)
            ov = out.rearrange("(t p) d -> p t d", p=P)
            expert_sync(sp, 0, 0)
            expert_sync(sp, 1, 1)
            attention_sync(sp)
            expert_sync(sp, 2, 0)
            expert_sync(sp, 3, 1)
            for h in range(HALVES):
                for c in range(GC):
                    tiles = slice(h * TH + c * TH // GC, h * TH + (c + 1) * TH // GC)
                    sp.wait_ge(s_comb, GC * (HALVES + h) + c + 1)
                    sp.dma_start(ov[:, tiles, :], X[:, tiles, :]).then_inc(s_out, 16)
            sp.wait_ge(s_out, 16 * HALVES * GC)

        @block.gpsimd
        def _(pool):
            pool.memset(zeros[:], 0.0).then_inc(s_zero, 1)
            pool.memset(half_power[:], -0.5).then_inc(s_zero, 1)
            pool.memset(hid[:, :, HIDDEN:HP], 0.0).then_inc(s_zero, 1)
            pool.wait_ge(s_zero, 3)
            pool.memset(W2[HIDDEN % P:P, :, HC - 1, :], 0.0).then_inc(s_zero, 1)
            pool.wait_ge(s_zero, 4)
            root_gpsimd(pool, 0)
            root_gpsimd(pool, 1)
            scatter_gpsimd(pool, 0, 0)
            scatter_gpsimd(pool, 1, 1)
            gather_gpsimd(pool, 0, 0)
            root_gpsimd(pool, 2)
            gather_gpsimd(pool, 1, 1)
            root_gpsimd(pool, 3)
            root_gpsimd(pool, 4)
            scatter_gpsimd(pool, 2, 0)
            root_gpsimd(pool, 5)
            scatter_gpsimd(pool, 3, 1)
            gather_gpsimd(pool, 2, 0)
            gather_gpsimd(pool, 3, 1)

        def none(i):
            return 0

        def late(i):
            return int(i >= 22)

        def often(i):
            return 0 if i < 0 else 2 if i < NT // 2 else 3

        def in_attention(i):
            if i < PAIRS * (NB + 1):
                return int(i >= 2 * PAIRS)
            return 2 if i >= 0 else 0

        def idle(ticks):
            for _ in range(ticks):
                yield

        @block.scalar
        def _(act):
            for g in range(HALVES):
                for _ in route_scalar(act, g):
                    pass
            expert_scalar(act, 0, idle(0), none)
            expert_scalar(act, 1, idle(0), none)
            side = chained(idle(SIDE), route_scalar(act, 2))
            attention_scalar(act, side, in_attention)
            for _ in side:
                pass
            side = route_scalar(act, 3)
            expert_scalar(act, 2, side, often)
            expert_scalar(act, 3, side, none)

        @block.tensor
        def _(pe):
            pe.wait_ge(s_const, 48)
            for g in range(HALVES):
                for _ in route_tensor(pe, g):
                    pass
            pe.wait_ge(s_zero, 4)
            expert_tensor(pe, 0, 0, idle(0), none)
            expert_tensor(pe, 1, 1, idle(0), none)
            pe.wait_ge(s_wa, 64)
            pe.wait_ge(s_vzero, 9)
            pe.wait_ge(s_ye, 2 * NT)
            pe.wait_ge(s_hte, 2 * NT)
            side = chained(idle(SIDE), route_tensor(pe, 2))
            attention_tensor(pe, side, in_attention)
            for _ in side:
                pass
            pe.wait_ge(s_exp2, 2 * PAIRS * BATCH)
            pe.wait_ge(s_ove, 2 * BATCH)
            pe.wait_ge(s_add, BATCH)
            side = route_tensor(pe, 3)
            expert_tensor(pe, 2, 0, side, often)
            expert_tensor(pe, 3, 1, side, none)

        @block.vector
        def _(dve):
            dve.wait_ge(s_const, 48)
            dve.wait_ge(s_x[0], 16)
            for _ in route_norm(dve, 0, 0):
                pass
            side = route_norm(dve, 1, 1)
            for step, _ in enumerate(route_vector(dve, 0, 0)):
                if step == 0:
                    dve.wait_ge(s_x[1], 16)
                next(side, None)
            for _ in route_vector(dve, 1, 1):
                pass
            for q in range(2):
                dve.memset(QS[q][:].rearrange("p r e n -> p (r e n)").bitcast(F32), 0.0).then_inc(s_vzero, 1)
                dve.memset(KS[q][STACK // 32 * 32:P], 1.0).then_inc(s_vzero, 1)
            for q in range(4):
                dve.memset(V1[q][:, :, :, HD:32], 0.0).then_inc(s_vzero, 1)
            dve.memset(zrows[:], 0.0).then_inc(s_vzero, 1)
            dve.wait_ge(s_vzero, 9)
            for q in range(4):
                link(dve, dve.memset(V1[q][:, :, :, HD:HD + 1], 1.0))
            link(dve, dve.tensor_copy(identb[:], ident))
            expert_vector(dve, 0, idle(0), none)
            side = chained(combine_vector(dve, 0, 0), norm_of_attention(dve, 0, 2))
            expert_vector(dve, 1, side, late)
            for _ in side:
                pass
            side = chained(combine_vector(dve, 1, 1), norm_of_attention(dve, 1, 3),
                           idle(SIDE - 2 * GC - TH // 4 - 4), route_norm(dve, 4, 0),
                           route_vector(dve, 2, 0))
            attention_vector(dve, side, in_attention)
            for _ in side:
                pass
            dve.wait_ge(s_add, BATCH)
            side = chained(route_norm(dve, 5, 1), route_vector(dve, 3, 1))
            expert_vector(dve, 2, side, often)
            for _ in side:
                pass
            expert_vector(dve, 3, idle(0), none)
            for h in range(HALVES):
                for _ in combine_vector(dve, 2 + h, h):
                    pass


def chained(*programs):
    for p in programs:
        yield from p


def kernel(L0_attn_hidden_states, L0_attn_Wq, L0_attn_Wk, L0_attn_Wv, L0_attn_Wo, L0_ffn_gate_w,
           L0_ffn_expert_bias, L0_ffn_w1, L0_ffn_w2, L0_ffn_w3):
    import concourse.bacc as bacc
    from concourse.bass_utils import run_bass_kernel_spmd

    def turned(w):
        return np.ascontiguousarray(np.asarray(w).T)

    def by_parity(w):
        w = np.asarray(w).reshape(PAIRS, 2, HD, D)
        return np.ascontiguousarray(w.transpose(3, 1, 0, 2).reshape(D, D))

    arrays = {
        "x": np.ascontiguousarray(L0_attn_hidden_states).reshape(BATCH * SEQ, D),
        "wq": by_parity(L0_attn_Wq), "wk": by_parity(L0_attn_Wk),
        "wv": turned(L0_attn_Wv), "wo": turned(L0_attn_Wo),
        "gate": turned(L0_ffn_gate_w), "bias": np.ascontiguousarray(L0_ffn_expert_bias),
        "w1": np.ascontiguousarray(L0_ffn_w1), "w2": np.ascontiguousarray(L0_ffn_w2),
        "w3": np.ascontiguousarray(L0_ffn_w3), "consts": constants(),
    }
    nc = bacc.Bacc("TRN2", target_bir_lowering=False, num_devices=1)
    aps = {n: nc.dram_tensor(f"in_{n}", a.shape, mybir.dt.from_np(a.dtype), kind="ExternalInput").ap()
           for n, a in arrays.items()}
    out = nc.dram_tensor("out_0", [BATCH * SEQ, D], F32, kind="ExternalOutput").ap()
    build(nc, *aps.values(), out)
    r = run_bass_kernel_spmd(nc, [{f"in_{n}": a for n, a in arrays.items()}], core_ids=[0])
    return r.results[0]["out_0"].reshape(BATCH, SEQ, D)
```
